# Optimizing a Trainium2 kernel written in Bass

```python
import numpy as np
import jax
import jax.numpy as jnp

def _softmax(x, axis=-1):
    return jax.nn.softmax(x, axis=axis)

def _gelu(x):
    return jax.nn.gelu(x, approximate=True)

def _silu(x):
    return jax.nn.silu(x)

def _sigmoid(x):
    return jax.nn.sigmoid(x)

def _layernorm(x, axis=-1, eps=1e-05):
    m = jnp.mean(x, axis=axis, keepdims=True)
    v = jnp.var(x, axis=axis, keepdims=True)
    return (x - m) / jnp.sqrt(v + eps)

def _scatter_add(tgt, idx, src, axis=0):
    return tgt.at[idx].add(src)

def _segment_sum(src, seg, n):
    return jax.ops.segment_sum(src, seg, n)
kernel_name = 'mk_xattn_ffn_d2_seqx_r8_264647'

def setup_inputs(seed: int=0):
    np.random.seed(seed)
    _w = jnp.asarray

    def _rec_inputs():
        import jax
        import jax.numpy as jnp
        _rk = jax.random.key(seed)
        x = 2.818e-05 + 1 * jax.random.normal(jax.random.fold_in(_rk, 1), (4, 256, 256), jnp.float32)
        _lenS = 256 - jax.random.randint(jax.random.fold_in(_rk, 7), (4,), 0, max(1, 256 // 4) + 1, jnp.int32)
        _lenS2 = 256 - jax.random.randint(jax.random.fold_in(_rk, 8), (4,), 0, max(1, 256 // 4) + 1, jnp.int32)
        _ctx_1024P = jax.random.normal(jax.random.fold_in(_rk, 11), (4, 16, 128), jnp.float32)
        _ctx_1024c = jax.random.dirichlet(jax.random.fold_in(_rk, 511), 0.3 * jnp.ones((16,), jnp.float32), (4, 256))
        _ctx_1024t = jnp.einsum('bsk,bkd->bsd', _ctx_1024c, _ctx_1024P)
        _ctx_1024t = _ctx_1024t * jax.lax.rsqrt(jnp.mean(jnp.square(_ctx_1024t)) + 1e-12) * 0.953939
        ctx_1024 = 7.22013e-05 + 1.00017 * (_ctx_1024t + 0.3 * jax.random.normal(jax.random.fold_in(_rk, 611), (4, 256, 128), jnp.float32))
        return (x, ctx_1024)
    x, ctx_1024 = _rec_inputs()

    def _L0_xattn_setup():
        import jax, jax.numpy as jnp
        import numpy as np
        B_, L_, D_MODEL = (4, 256, 128)
        D_STATE, D_CONV, EXPAND = (16, 4, 2)
        D_INNER = EXPAND * D_MODEL
        DT_RANK = (D_MODEL + 15) // 16

        def silu(x):
            return x * jax.nn.sigmoid(x)
        key = jax.random.key(seed)
        ks = jax.random.split(key, 10)
        f32 = jnp.float32
        hidden_states = jax.random.normal(ks[0], (B_, L_, D_MODEL), dtype=f32)
        z = jax.random.normal(ks[1], (B_, D_INNER, L_), dtype=f32)
        in_proj_w = jax.random.normal(ks[2], (D_INNER, D_MODEL), dtype=f32) * 0.02
        conv_w = jax.random.normal(ks[3], (D_INNER, 1, D_CONV), dtype=f32) * 0.1
        conv_b = jax.random.normal(ks[4], (D_INNER,), dtype=f32) * 0.02
        x_proj_w = jax.random.normal(ks[5], (DT_RANK + 2 * D_STATE, D_INNER), dtype=f32) * 0.02
        dt_proj_w = jax.random.uniform(ks[6], (D_INNER, DT_RANK), dtype=f32, minval=-DT_RANK ** (-0.5), maxval=DT_RANK ** (-0.5))
        dt = jnp.exp(jax.random.uniform(ks[7], (D_INNER,), dtype=f32, minval=np.log(0.001), maxval=np.log(0.1)))
        dt_proj_b = jnp.log(jnp.expm1(dt))
        A_log = jnp.log(jnp.broadcast_to(jnp.arange(1, D_STATE + 1, dtype=f32), (D_INNER, D_STATE)))
        D = jnp.ones((D_INNER,), f32)
        return {'hidden_states': hidden_states, 'z': z, 'in_proj_w': in_proj_w, 'conv_w': conv_w, 'conv_b': conv_b, 'x_proj_w': x_proj_w, 'dt_proj_w': dt_proj_w, 'dt_proj_b': dt_proj_b, 'A_log': A_log, 'D': D}
    _L0_xattn_all = _L0_xattn_setup()
    _L0_xattn_in = {k: v for k, v in _L0_xattn_all.items() if k in ('in_proj_w', 'conv_w', 'conv_b', 'x_proj_w', 'dt_proj_w', 'dt_proj_b', 'A_log', 'D')}
    del _L0_xattn_all

    def _L0_ffn_setup():
        import jax, jax.numpy as jnp
        import numpy as np
        ACT_BITS = 8
        EPS = 1e-05

        def act_quant(x, bits=ACT_BITS):
            qb = float(2 ** (bits - 1))
            scale = qb / jnp.clip(jnp.max(jnp.abs(x), axis=-1, keepdims=True), EPS)
            xq = jnp.clip(jnp.round(x * scale), -qb, qb - 1) / scale
            return x + jax.lax.stop_gradient(xq - x)

        def weight_quant(w):
            scale = 1.0 / jnp.clip(jnp.mean(jnp.abs(w)), EPS)
            wq = jnp.clip(jnp.round(w * scale), -1.0, 1.0) / scale
            return w + jax.lax.stop_gradient(wq - w)

        def fwht(x):
            shape = x.shape
            n = shape[-1]
            x = x.reshape(-1, n)
            h = 1
            while h < n:
                x = x.reshape(-1, n // (2 * h), 2, h)
                a, b = (x[..., 0, :], x[..., 1, :])
                x = jnp.stack([a + b, a - b], axis=-2).reshape(-1, n)
                h *= 2
            return (x * (1.0 / np.sqrt(n)).astype(np.float32)).reshape(shape)

        def bitlinear(x, w):
            return jnp.einsum('bsh,oh->bso', act_quant(x), weight_quant(w))

        def h_bitlinear(x, w):
            return jnp.einsum('bsh,oh->bso', act_quant(fwht(x)), weight_quant(w))
        key = jax.random.key(seed)
        k1, k2, k3, k4 = jax.random.split(key, 4)
        H, I = (256, 1024)
        B, S = (4, 256)
        std_in = 1.0 / np.sqrt(H)
        std_mid = 1.0 / np.sqrt(I)
        return {'x': jax.random.normal(k1, (B, S, H), dtype=jnp.float32), 'w_gate': jax.random.normal(k2, (I, H), dtype=jnp.float32) * std_in, 'w_up': jax.random.normal(k3, (I, H), dtype=jnp.float32) * std_in, 'w_down': jax.random.normal(k4, (H, I), dtype=jnp.float32) * std_mid}
    _L0_ffn_all = _L0_ffn_setup()
    _L0_ffn_in = {k: v for k, v in _L0_ffn_all.items() if k in ('w_gate', 'w_up', 'w_down')}
    del _L0_ffn_all

    def _L1_xattn_setup():
        import jax, jax.numpy as jnp
        import numpy as np
        key = jax.random.key(seed)
        ks = jax.random.split(key, 6)
        B, L, N, C, D = (8, 64, 256, 128, 128)
        return {'teacher_logits': jax.random.normal(ks[0], (B, L, N), dtype=jnp.float32), 'teacher_features': jax.random.normal(ks[1], (B, N, C), dtype=jnp.float32), 'Wq': jax.random.normal(ks[2], (D, C), dtype=jnp.float32) * (1.0 / np.sqrt(C)), 'bq': jnp.zeros((D,), dtype=jnp.float32), 'Wk': jax.random.normal(ks[3], (D, C), dtype=jnp.float32) * (1.0 / np.sqrt(C)), 'bk': jnp.zeros((D,), dtype=jnp.float32)}
    _L1_xattn_all = _L1_xattn_setup()
    _L1_xattn_in = {k: v for k, v in _L1_xattn_all.items() if k in ('Wq', 'bq', 'Wk', 'bk')}
    del _L1_xattn_all

    def _L1_ffn_setup():
        import jax, jax.numpy as jnp
        import numpy as np
        EPS = 1e-06
        Q_B = 128.0

        def layer_norm(x):
            mean = jnp.mean(x, axis=-1, keepdims=True)
            var = jnp.var(x, axis=-1, keepdims=True)
            return (x - mean) / jnp.sqrt(var + EPS)

        def absmax_quant(x):
            gamma = jnp.max(jnp.abs(x), axis=-1, keepdims=True)
            x_hat = jnp.clip(x * Q_B / gamma, -Q_B + EPS, Q_B - EPS)
            return x_hat * gamma / Q_B

        def ternarize_weights(w):
            gamma = jnp.mean(jnp.abs(w))
            return jnp.sign(jnp.round(w / (gamma + EPS))) * gamma

        def bitlinear(x, w):
            xn = layer_norm(x)
            x_hat = xn + jax.lax.stop_gradient(absmax_quant(xn) - xn)
            w_hat = w + jax.lax.stop_gradient(ternarize_weights(w) - w)
            return jnp.einsum('bsd,od->bso', x_hat, w_hat)
        key = jax.random.key(seed)
        k1, k2, k3 = jax.random.split(key, 3)
        B, S, D = (4, 256, 256)
        x = jax.random.normal(k1, (B, S, D), dtype=jnp.float32)
        w_fc = jax.random.normal(k2, (4 * D, D), dtype=jnp.float32) / np.sqrt(D)
        w_proj = jax.random.normal(k3, (D, 4 * D), dtype=jnp.float32) / np.sqrt(4 * D)
        return {'x': x, 'w_fc': w_fc, 'w_proj': w_proj}
    _L1_ffn_all = _L1_ffn_setup()
    _L1_ffn_in = {k: v for k, v in _L1_ffn_all.items() if k in ('w_fc', 'w_proj')}
    del _L1_ffn_all
    return {'x': x, 'ctx_1024': ctx_1024, 'L0_xattn_in_proj_w': _L0_xattn_in['in_proj_w'], 'L0_xattn_conv_w': _L0_xattn_in['conv_w'], 'L0_xattn_conv_b': _L0_xattn_in['conv_b'], 'L0_xattn_x_proj_w': _L0_xattn_in['x_proj_w'], 'L0_xattn_dt_proj_w': _L0_xattn_in['dt_proj_w'], 'L0_xattn_dt_proj_b': _L0_xattn_in['dt_proj_b'], 'L0_xattn_A_log': _L0_xattn_in['A_log'], 'L0_xattn_D': _L0_xattn_in['D'], 'L0_ffn_w_gate': _L0_ffn_in['w_gate'], 'L0_ffn_w_up': _L0_ffn_in['w_up'], 'L0_ffn_w_down': _L0_ffn_in['w_down'], 'L1_xattn_Wq': _L1_xattn_in['Wq'], 'L1_xattn_bq': _L1_xattn_in['bq'], 'L1_xattn_Wk': _L1_xattn_in['Wk'], 'L1_xattn_bk': _L1_xattn_in['bk'], 'L1_ffn_w_fc': _L1_ffn_in['w_fc'], 'L1_ffn_w_proj': _L1_ffn_in['w_proj']}

def reference(x, ctx_1024, L0_xattn_in_proj_w, L0_xattn_conv_w, L0_xattn_conv_b, L0_xattn_x_proj_w, L0_xattn_dt_proj_w, L0_xattn_dt_proj_b, L0_xattn_A_log, L0_xattn_D, L0_ffn_w_gate, L0_ffn_w_up, L0_ffn_w_down, L1_xattn_Wq, L1_xattn_bq, L1_xattn_Wk, L1_xattn_bk, L1_ffn_w_fc, L1_ffn_w_proj):
    import jax
    import jax.numpy as jnp

    def _L0_xattn_ref(hidden_states, z, in_proj_w, conv_w, conv_b, x_proj_w, dt_proj_w, dt_proj_b, A_log, D):
        import jax, jax.numpy as jnp
        import numpy as np
        B_, L_, D_MODEL = (4, 256, 128)
        D_STATE, D_CONV, EXPAND = (16, 4, 2)
        D_INNER = EXPAND * D_MODEL
        DT_RANK = (D_MODEL + 15) // 16

        def silu(x):
            return x * jax.nn.sigmoid(x)
        Bsz, L, _ = hidden_states.shape
        d_inner, _, d_conv = conv_w.shape
        dt_rank = dt_proj_w.shape[1]
        d_state = A_log.shape[1]
        x = jnp.einsum('bld,ed->bel', hidden_states, in_proj_w)
        xc = jax.lax.conv_general_dilated(x, conv_w, window_strides=(1,), padding=[(d_conv - 1, 0)], feature_group_count=d_inner, dimension_numbers=('NCH', 'OIH', 'NCH'))
        x = silu(xc + conv_b[None, :, None])
        x_dbl = jnp.einsum('bdl,ed->bel', x, x_proj_w)
        dt_low, Bm, Cm = jnp.split(x_dbl, [dt_rank, dt_rank + d_state], axis=1)
        dt = jnp.einsum('brl,dr->bdl', dt_low, dt_proj_w)
        dt = jax.nn.softplus(dt + dt_proj_b[None, :, None])
        A = -jnp.exp(A_log)
        dt_t = jnp.moveaxis(dt, -1, 0)
        B_t = jnp.moveaxis(Bm, -1, 0)
        C_t = jnp.moveaxis(Cm, -1, 0)
        u_t = jnp.moveaxis(x, -1, 0)

        def step(state, inp):
            d, b, c, u = inp
            dA = jnp.exp(d[..., None] * A)
            state = state * dA + (d * u)[..., None] * b[:, None, :]
            y = jnp.einsum('bdn,bn->bd', state, c)
            return (state, y)
        state0 = jnp.zeros((Bsz, d_inner, d_state), x.dtype)
        _, ys = jax.lax.scan(step, state0, (dt_t, B_t, C_t, u_t))
        y = jnp.moveaxis(ys, 0, 2)
        y = y + D[None, :, None] * x
        y = y * silu(z)
        return jnp.swapaxes(y, 1, 2)

    def _L0_ffn_ref(x, w_gate, w_up, w_down):
        import jax, jax.numpy as jnp
        import numpy as np
        ACT_BITS = 8
        EPS = 1e-05

        def act_quant(x, bits=ACT_BITS):
            qb = float(2 ** (bits - 1))
            scale = qb / jnp.clip(jnp.max(jnp.abs(x), axis=-1, keepdims=True), EPS)
            xq = jnp.clip(jnp.round(x * scale), -qb, qb - 1) / scale
            return x + jax.lax.stop_gradient(xq - x)

        def weight_quant(w):
            scale = 1.0 / jnp.clip(jnp.mean(jnp.abs(w)), EPS)
            wq = jnp.clip(jnp.round(w * scale), -1.0, 1.0) / scale
            return w + jax.lax.stop_gradient(wq - w)

        def fwht(x):
            shape = x.shape
            n = shape[-1]
            x = x.reshape(-1, n)
            h = 1
            while h < n:
                x = x.reshape(-1, n // (2 * h), 2, h)
                a, b = (x[..., 0, :], x[..., 1, :])
                x = jnp.stack([a + b, a - b], axis=-2).reshape(-1, n)
                h *= 2
            return (x * (1.0 / np.sqrt(n)).astype(np.float32)).reshape(shape)

        def bitlinear(x, w):
            return jnp.einsum('bsh,oh->bso', act_quant(x), weight_quant(w))

        def h_bitlinear(x, w):
            return jnp.einsum('bsh,oh->bso', act_quant(fwht(x)), weight_quant(w))
        gate = bitlinear(x, w_gate)
        up = bitlinear(x, w_up)
        intermediate = jax.nn.silu(gate) * up
        return h_bitlinear(intermediate, w_down)

    def _L1_xattn_ref(teacher_logits, teacher_features, Wq, bq, Wk, bk):
        import jax, jax.numpy as jnp
        import numpy as np
        query = jnp.einsum('bnc,dc->bnd', teacher_features, Wq) + bq
        key = jnp.einsum('bnc,dc->bnd', teacher_features, Wk) + bk
        energy = jnp.einsum('bnd,bmd->bnm', query, key)
        attention = jax.nn.softmax(energy, axis=-1)
        x_m = jnp.einsum('bln,bmn->blm', teacher_logits, attention)
        return x_m

    def _L1_ffn_ref(x, w_fc, w_proj):
        import jax, jax.numpy as jnp
        import numpy as np
        EPS = 1e-06
        Q_B = 128.0

        def layer_norm(x):
            mean = jnp.mean(x, axis=-1, keepdims=True)
            var = jnp.var(x, axis=-1, keepdims=True)
            return (x - mean) / jnp.sqrt(var + EPS)

        def absmax_quant(x):
            gamma = jnp.max(jnp.abs(x), axis=-1, keepdims=True)
            x_hat = jnp.clip(x * Q_B / gamma, -Q_B + EPS, Q_B - EPS)
            return x_hat * gamma / Q_B

        def ternarize_weights(w):
            gamma = jnp.mean(jnp.abs(w))
            return jnp.sign(jnp.round(w / (gamma + EPS))) * gamma

        def bitlinear(x, w):
            xn = layer_norm(x)
            x_hat = xn + jax.lax.stop_gradient(absmax_quant(xn) - xn)
            w_hat = w + jax.lax.stop_gradient(ternarize_weights(w) - w)
            return jnp.einsum('bsd,od->bso', x_hat, w_hat)
        h = bitlinear(x, w_fc)
        h = jax.nn.gelu(h, approximate=False)
        return bitlinear(h, w_proj)
    x = x + _L0_xattn_ref(ctx_1024, _layernorm(x, axis=-1), L0_xattn_in_proj_w, L0_xattn_conv_w, L0_xattn_conv_b, L0_xattn_x_proj_w, L0_xattn_dt_proj_w, L0_xattn_dt_proj_b, L0_xattn_A_log, L0_xattn_D)
    x = x + _L0_ffn_ref(_layernorm(x, axis=-1), L0_ffn_w_gate, L0_ffn_w_up, L0_ffn_w_down)
    x = x + _L1_xattn_ref(_layernorm(x, axis=-1), ctx_1024, L1_xattn_Wq, L1_xattn_bq, L1_xattn_Wk, L1_xattn_bk)
    x = x + _L1_ffn_ref(_layernorm(x, axis=-1), L1_ffn_w_fc, L1_ffn_w_proj)
    return x

_drawn_inputs = setup_inputs


def setup_inputs(seed=0):
    import zlib

    import numpy as np

    out = dict(_drawn_inputs(seed))
    spreads = {'L0_xattn_D': (1.0, 0.6), 'L1_xattn_bq': (0.0, 0.1), 'L1_xattn_bk': (0.0, 0.8)}
    factors = {'L0_xattn_in_proj_w': 4.063,
     'L0_xattn_conv_w': 4.374,
     'L0_xattn_conv_b': 8.0,
     'L0_xattn_x_proj_w': 8.0,
     'L0_xattn_dt_proj_w': 8.0,
     'L0_xattn_dt_proj_b': 8.0,
     'L0_xattn_A_log': 8.0}
    for name, (base, spread) in spreads.items():
        noise = np.random.default_rng([zlib.crc32(name.encode()), seed]).standard_normal(out[name].shape)
        drawn = base * np.exp(spread * noise) if base else spread * noise
        out[name] = jnp.asarray(drawn.astype(out[name].dtype))
    for name, factor in factors.items():
        out[name] = (out[name] * factor).astype(out[name].dtype)
    return out
```

```python
from contextlib import ExitStack

import numpy as np

import concourse.bass as bass
from concourse import mybir

F32 = mybir.dt.float32
BF16 = mybir.dt.bfloat16
ALU = mybir.AluOpType
ACT = mybir.ActivationFunctionType
AX = mybir.AxisListType

P = 128
B, L, D = 4, 256, 256
T = L // P
C = 128
NST = 16
TAPS = 4
RANK = 8
FF = 1024
NQ = 4
QUADS = NST // NQ
STEPS = QUADS * T
SPOTS = 3 * STEPS
ROUND = 12582912.0
QB = 128.0
EPS0 = 1e-5
EPS1 = 1e-6
G8 = FF // P


def build(nc, x, ctxT, inproj, convw, convb, xprojT, dtprojT, dtb, alog, dskip, wgate, wup, wdown,
          wq, wk, bq, bk, wfc, wproj, eye, had, sel, out):
    with ExitStack() as ctx:
        def sb(name, shape, dt=F32):
            return ctx.enter_context(nc.sbuf_tensor(name, shape, dt))

        def ps(name):
            return ctx.enter_context(nc.psum_tensor(name, [P, 512], F32))

        def sem(name):
            return ctx.enter_context(nc.semaphore(name))

        X = sb("X", [P, B, T, D])
        CT = sb("CT", [P, B, TAPS - 1 + L])
        INW = sb("INW", [P, D])
        WCONV = sb("WCONV", [P, TAPS, D])
        XPW = sb("XPW", [P, T, 104])
        DTW = sb("DTW", [104, D])
        VEC = sb("VEC", [P, 3, T])
        HALF = sb("HALF", [P, 2, T])
        ALOG = sb("ALOG", [P, T, NST])
        AEXP = sb("AEXP", [P, T, NST])
        ANEG = sb("ANEG", [P, T, NST])
        WQK = sb("WQK", [P, 2, C])
        BQK = sb("BQK", [P, 2])
        EYE = sb("EYE", [P, P])
        EYEB = sb("EYEB", [P, P], BF16)
        HAD = sb("HAD", [P, 2, 2 * P])
        SELC = sb("SELC", [96, 32], BF16)
        SEL = sb("SEL", [96, 32, P], BF16)
        ONES = sb("ONES", [P, P])
        MHALF = sb("MHALF", [P, 4])
        WFC = sb("WFC", [P, 2, FF])
        WPR = sb("WPR", [P, G8, D])
        WG = sb("WG", [P, 2, FF], BF16)
        WU = sb("WU", [P, 2, FF], BF16)
        WD = sb("WD", [P, G8, D], BF16)
        ROUNDC = sb("ROUNDC", [P, 1])
        WSUM = sb("WSUM", [P, 5])
        WMEAN = sb("WMEAN", [P, 5])
        WDIV = sb("WDIV", [P, 5])
        WREC = sb("WREC", [P, 5])
        WSC = sb("WSC", [P, 4])

        CACC = sb("CACC", [P, T, L])
        TH = sb("TH", [P, T, L])
        U2 = sb("U2", [P, 2, T, L])
        XD = sb("XD", [104, L])
        PARTS = sb("PARTS", [96, 2, L], BF16)
        EB, WB = CACC, TH
        LNB = sb("LNB", [P, T, L])
        RES = sb("RES", [P, T, L])
        R1 = RES[0:96, 0, :]
        RELU = sb("RELU", [P, T, L])
        DT = sb("DT", [P, 2, T, L])
        DTU = sb("DTU", [P, 2, T, L])
        ZN = sb("ZN", [P, T, L])
        ZTH = sb("ZTH", [P, T, L])
        SZ = sb("SZ", [P, 2, T, L])
        NDA, NH, NZ = 3, 2, 4
        DA = sb("DA", [P, NDA, NQ, L])
        H = sb("H", [P, NH, NQ, L])
        Z = sb("Z", [P, NZ, NQ, L])
        CW = Z[:, 0, :, :]
        ACC = sb("ACC", [P, T, NQ, L])
        FOLD = sb("FOLD", [P, T, 2, L])
        YS = sb("YS", [P, T, L])
        V2 = sb("V2", [P, T, L])

        XR = sb("XR", [P, T, D])
        X1 = X2 = X3 = XR
        XO = sb("XO", [P, 2, T, D])

        STT = sb("STT", [P, 4, T, 6])
        MV = sb("MV", [P, 4, T, 2])
        VE = sb("VE", [P, 4, T])
        RS = sb("RS", [P, 4, T])

        XN = sb("XN", [P, T, D])
        XQ = sb("XQ", [P, T, D])
        XN2, D3, C3 = XN, XN, XQ
        Q1 = sb("Q1", [P, T, D], BF16)
        QT = sb("QT", [P, T, 2, P], BF16)
        AM = sb("AM", [P, T])
        AMC = sb("AMC", [P, T])
        RC = sb("RC", [P, T])
        QS = sb("QS", [P, T])
        GAH = sb("GAH", [P, T])
        KA = sb("KA", [P, T])
        KK = sb("KK", [P, T])
        TG = sb("TG", [P, 2, 512])
        SG = sb("SG", [P, 2, 512])
        XM = sb("XM", [P, T, G8, P])
        HA = sb("HA", [P, T, G8, P])
        HB = sb("HB", [P, T, G8, P])
        XTS = sb("XTS", [P, T, G8, P])
        AM2 = sb("AM2", [P, T, 2])
        AMX = sb("AMX", [P, T])
        AMT = sb("AMT", [P, T])
        RC2 = sb("RC2", [P, T])
        QS2 = sb("QS2", [P, T])
        DSC = sb("DSC", [P, T])
        YQ = XM[:, :, :, :].rearrange("p t c l -> p t (c l)")
        Q2 = HA[:, 0, :, :].rearrange("p c l -> p (c l)").bitcast(BF16).rearrange("p (t f) -> p t f", t=T)
        Q2T = HA[:, 1, :, :].rearrange("p c l -> p (c l)").bitcast(BF16).rearrange("p (t c l) -> p t c l", t=T, c=G8)

        QK = sb("QK", [P, 2, L])
        NMX = sb("NMX", [P, T])
        EX = sb("EX", [P, T, L])
        RSUM = sb("RSUM", [P, T])
        RINV = sb("RINV", [P, T])
        PN = EX
        AT = sb("AT", [P, 2, T, L])
        X2T = sb("X2T", [P, T, T, P])

        GM = sb("GM", [P, T])
        GI = sb("GI", [P, T])
        GN = sb("GN", [P, T])
        S1 = sb("S1", [P, T])
        X3T = X2T
        HG = XM[:, :, :, :].rearrange("p t c l -> p t (c l)")
        ST3 = sb("ST3", [P, T, 2, 6])
        MV3 = sb("MV3", [P, T, 2])
        VE3 = sb("VE3", [P, T])
        RS3 = sb("RS3", [P, T])
        MR3 = sb("MR3", [P, T])
        HD = HA[:, :, :, :].rearrange("p t c l -> p t (c l)")
        GM2 = sb("GM2", [P, T])
        NG2 = sb("NG2", [P, T])
        GI2 = sb("GI2", [P, T])
        GN2 = sb("GN2", [P, T])
        S2 = sb("S2", [P, T])
        NG = sb("NG", [P, T])
        HC = HB[:, :, :, :].rearrange("p t c l -> p t (c l)")
        HT = XTS
        WRAW = [w[:, :, :, :].rearrange("p t c l -> p (t c l)") for w in (XM, HA, HB)]
        WABS = XTS[:, :, :, :].rearrange("p t c l -> p (t c l)")

        BB = ctx.enter_context(nc.psum_tensor("BB", [P, NQ, L], F32))
        CB = ctx.enter_context(nc.psum_tensor("CB", [P, NQ, L], F32))
        PA = ps("PA")
        R = [ps("R0"), ps("R1"), ps("R2")]

        d_ctx = [sem(f"d_ctx{b}") for b in range(B)]
        d_x = [sem(f"d_x{b}") for b in range(B)]
        d_in, d_cw, d_xp, d_dtw, d_vec, d_alog = (sem(n) for n in (
            "d_in", "d_cw", "d_xp", "d_dtw", "d_vec", "d_alog"))
        d_qk, d_eye, d_had, d_sel = (sem(n) for n in ("d_qk", "d_eye", "d_had", "d_sel"))
        d_w = [sem(f"d_w{i}") for i in range(5)]
        d_out = [sem(f"d_out{b}") for b in range(B)]
        s_const = sem("s_const")
        s_wconv = sem("s_wconv")
        s_aneg = sem("s_aneg")
        s_aexp = sem("s_aexp")
        s_mhalf = sem("s_mhalf")
        s_eyeb = sem("s_eyeb")
        s_sel = sem("s_sel")
        s_wabs = sem("s_wabs")
        s_wtot = sem("s_wtot")
        s_wsc = sem("s_wsc")
        s_wrnd = sem("s_wrnd")
        s_wter = sem("s_wter")

        s_conv = sem("s_conv")
        s_act = sem("s_act")
        s_u = sem("s_u")
        s_xdbl = sem("s_xdbl")
        s_xd = sem("s_xd")
        s_dtp = sem("s_dtp")
        s_parts = sem("s_parts")
        s_ax = sem("s_ax")
        s_e = sem("s_e")
        s_relu = sem("s_relu")
        s_w1e = sem("s_w1e")
        s_ln = sem("s_ln")
        s_res = sem("s_res")
        s_dt = sem("s_dt")
        s_lnst = [sem(f"s_lnst{i}") for i in range(4)]
        s_rstd = [sem(f"s_rstd{i}") for i in range(4)]
        s_zn = sem("s_zn")
        s_zth = sem("s_zth")
        s_sz = sem("s_sz")

        s_bb = sem("s_bb")
        s_cb = sem("s_cb")
        s_da = sem("s_da")
        s_dbu = sem("s_dbu")
        s_scan = sem("s_scan")
        s_z = sem("s_z")
        s_acc = sem("s_acc")
        s_fold = sem("s_fold")

        s_v = sem("s_v")
        s_yT = sem("s_yT")
        s_x1 = sem("s_x1")
        s_xn = sem("s_xn")
        s_am = sem("s_am")
        s_q1 = sem("s_q1")
        s_qT = sem("s_qT")
        s_qTs = sem("s_qTs")
        s_gu = sem("s_gu")
        s_tg = sem("s_tg")
        s_sg = sem("s_sg")
        s_xm = sem("s_xm")
        s_hA = sem("s_hA")
        s_hB = sem("s_hB")
        s_XT = sem("s_XT")
        s_XTs = sem("s_XTs")
        s_Y = sem("s_Y")
        s_am2 = sem("s_am2")
        s_qs2 = sem("s_qs2")
        s_yq = sem("s_yq")
        s_q2 = sem("s_q2")
        s_q2T = sem("s_q2T")
        s_q2Ts = sem("s_q2Ts")
        s_dn = sem("s_dn")
        s_x2 = sem("s_x2")

        s_pqk = sem("s_pqk")
        s_qk = sem("s_qk")
        s_en = sem("s_en")
        s_mx = sem("s_mx")
        s_ex = sem("s_ex")
        s_rinv = sem("s_rinv")
        s_pn = sem("s_pn")
        s_pT = sem("s_pT")
        s_AT = sem("s_AT")
        s_xn2 = sem("s_xn2")
        s_x2T = sem("s_x2T")
        s_x2Ts = sem("s_x2Ts")
        s_pxm = sem("s_pxm")
        s_x3 = sem("s_x3")

        s_d3 = sem("s_d3")
        s_gm = sem("s_gm")
        s_c3 = sem("s_c3")
        s_x3T = sem("s_x3T")
        s_x3Ts = sem("s_x3Ts")
        s_fc = sem("s_fc")
        s_h = sem("s_h")
        s_st3 = sem("s_st3")
        s_rs3 = sem("s_rs3")
        s_mr3 = sem("s_mr3")
        s_hd = sem("s_hd")
        s_gm2 = sem("s_gm2")
        s_hc = sem("s_hc")
        s_hT = sem("s_hT")
        s_hTs = sem("s_hTs")
        s_pj = sem("s_pj")
        s_o = sem("s_o")

        block = ctx.enter_context(nc.Block())

        @block.sync
        def _(sync):
            for b in range(B):
                sync.dma_start(CT[:, b, TAPS - 1:], ctxT[:, b, :]).then_inc(d_ctx[b], 16)
                if b == 0:
                    sync.dma_start(INW[:, :], inproj).then_inc(d_in, 16)
                    sync.dma_start(CW, convw.partition_broadcast(P)).then_inc(d_cw, 16)
                    sync.dma_start(VEC[:, 0, :], convb).then_inc(d_vec, 16)
                    sync.dma_start(VEC[:, 1, :], dtb).then_inc(d_vec, 16)
                    sync.dma_start(VEC[:, 2, :], dskip).then_inc(d_vec, 16)
                    sync.dma_start(XPW[:, :, :], xprojT).then_inc(d_xp, 16)
                    sync.dma_start(DTW[96:104, :], dtprojT).then_inc(d_dtw, 16)
                    sync.dma_start(ALOG[:, :, :], alog).then_inc(d_alog, 16)
                    sync.dma_start(SELC[:, :], sel).then_inc(d_sel, 16)
                sync.dma_start(X[:, b, :, :], x[:, b, :, :]).then_inc(d_x[b], 16)
            sync.dma_start(EYE[:, :], eye).then_inc(d_eye, 16)
            sync.dma_start(WQK[:, 0, :], wq).then_inc(d_qk, 16)
            sync.dma_start(WQK[:, 1, :], wk).then_inc(d_qk, 16)
            sync.dma_start(BQK[:, 0:1], bq).then_inc(d_qk, 16)
            sync.dma_start(BQK[:, 1:2], bk).then_inc(d_qk, 16)
            sync.dma_start(WRAW[0], wgate).then_inc(d_w[0], 16)
            sync.dma_start(WRAW[1], wup).then_inc(d_w[1], 16)
            sync.dma_start(WRAW[2], wdown).then_inc(d_w[2], 16)
            sync.dma_start(HAD[:, :, :], had).then_inc(d_had, 16)
            sync.dma_start(WFC[:, :, :], wfc).then_inc(d_w[3], 16)
            sync.dma_start(WPR[:, :, :], wproj).then_inc(d_w[4], 16)
            for b in range(B):
                for t in range(T):
                    sync.wait_ge(s_o, T * b + t + 1)
                    sync.dma_start(out[:, b, t, :], XO[:, b % 2, t, :]).then_inc(d_out[b], 16)
            for b in range(B):
                sync.wait_ge(d_out[b], 16 * T)

        @block.tensor
        def _(pe):
            def prep_conv(b):
                pe.wait_ge(d_ctx[b], 16)
                pe.wait_ge(s_wconv, 1)
                pe.wait_ge(s_const, 4)
                if b > 0:
                    pe.wait_ge(s_relu, 2 * b)
                    pe.wait_ge(s_ax, 2 * b)
                    if b > 1:
                        pe.wait_ge(s_AT, b - 1)
                for c in range(T):
                    for k in range(TAPS):
                        mm = pe.matmul(PA[:, c * L:(c + 1) * L], WCONV[:, k, c * P:(c + 1) * P],
                                       CT[:, b, k:k + L], start=(k == 0), stop=(k == TAPS - 1))
                mm.then_inc(s_conv, 1)

            def prep_xdbl(b):
                pe.wait_ge(s_u, b + 1)
                pe.wait_ge(d_xp, 16)
                for c in range(T):
                    mm = pe.matmul(PA[0:104, 0:L], XPW[:, c, :], U2[:, b % 2, c, :],
                                   start=(c == 0), stop=(c == T - 1))
                mm.then_inc(s_xdbl, 1)

            def prep_dt(b):
                pe.wait_ge(s_xd, b + 1)
                pe.wait_ge(d_dtw, 16)
                for c in range(T):
                    mm = pe.matmul(PA[:, c * L:(c + 1) * L], DTW[96:104, c * P:(c + 1) * P],
                                   XD[96:104, :], start=True, stop=True)
                mm.then_inc(s_dtp, 1)

            def bcast_b(b, q):
                if q == 0:
                    pe.wait_ge(s_parts, 4 * (b + 1))
                    pe.wait_ge(s_sel, 1)
                g = STEPS * b + T * q
                if g:
                    pe.wait_ge(s_dbu, g)
                for n in range(NQ):
                    mm = pe.matmul(BB[:, n, :], SEL[:, NQ * q + n, :],
                                   PARTS[:, b % 2, :], start=True, stop=True)
                mm.then_inc(s_bb, 1)

            def bcast_c(b, q):
                g = STEPS * b + T * q
                if g:
                    pe.wait_ge(s_z, g)
                for n in range(NQ):
                    mm = pe.matmul(CB[:, n, :], SEL[:, NST + NQ * q + n, :],
                                   PARTS[:, b % 2, :], start=True, stop=True)
                mm.then_inc(s_cb, 1)

            def attn_qk(b):
                pe.wait_ge(d_qk, 64)
                nb = min(b + 2, B)
                pe.wait_ge(s_relu, 2 * nb)
                pe.wait_ge(s_ax, 2 * nb)
                if b > 0:
                    pe.wait_ge(s_AT, b)
                for i in range(2):
                    mm = pe.matmul(PA[:, i * L:(i + 1) * L], WQK[:, i, :], CT[:, b, TAPS - 1:],
                                   start=True, stop=True)
                mm.then_inc(s_pqk, 1)

            def attn_energy(b):
                pe.wait_ge(s_qk, 2 * (b + 1))
                for t in range(T):
                    mm = pe.matmul(PA[:, t * L:(t + 1) * L], QK[:, 0, t * P:(t + 1) * P], QK[:, 1, :],
                                   start=True, stop=True)
                mm.then_inc(s_en, 1)

            def attn_turn(b):
                pe.wait_ge(s_pn, 2 * (b + 1))
                for c in range(T):
                    for t in range(T):
                        mm = pe.transpose(PA[:, c * L + t * P:c * L + (t + 1) * P],
                                          PN[:, t, c * P:(c + 1) * P], EYE[:, :])
                mm.then_inc(s_pT, 1)

            def weight_sums(first, n):
                pe.wait_ge(s_wabs, first + n)
                pe.wait_ge(s_const, 4)
                if first:
                    pe.wait_ge(s_wsc, 5)
                pe.matmul(R[0][:, 0:n], ONES[:, :], WSUM[:, first:first + n],
                          start=True, stop=True).then_inc(s_wtot, 1)

            def turn_y(b):
                pe.wait_ge(s_v, 3 * (b + 1))
                if b > 0:
                    pe.wait_ge(s_o, T * b)
                for t in range(T):
                    for c in range(T):
                        mm = pe.transpose(R[0][:, t * D + c * P:t * D + (c + 1) * P],
                                          V2[:, c, t * P:(t + 1) * P], EYE[:, :])
                mm.then_inc(s_yT, 1)

            def turn_q1(b):
                pe.wait_ge(s_q1, 3 * (b + 1))
                r = R[1][:, 0:256].bitcast(BF16)
                for t in range(T):
                    for k in range(2):
                        j = (t * 2 + k) * P
                        mm = pe.transpose(r[:, j:j + P], Q1[:, t, k * P:(k + 1) * P], EYEB[:, :])
                mm.then_inc(s_qT, 1)

            def gate_up(b, j):
                t, i = j // 2, j % 2
                if j == 0:
                    pe.wait_ge(s_qTs, b + 1)
                    if b == 0:
                        pe.wait_ge(s_wter, 4)
                    pe.wait_ge(s_x1, b + 1)
                    if b > 0:
                        pe.wait_ge(s_o, T * b)
                else:
                    pe.wait_ge(s_xm, 4 * b + j)
                g, u = R[(2 * j + 2) % 3], R[(2 * j + 3) % 3]
                for w, r in ((WG, g), (WU, u)):
                    for k in range(2):
                        mm = pe.matmul(r[:, :], QT[:, t, k, :], w[:, k, i * 512:(i + 1) * 512],
                                       start=(k == 0), stop=(k == 1))
                mm.then_inc(s_gu, 1)

            def turn_x(b, j):
                t, i = j // 2, j % 2
                pe.wait_ge(s_hB, 4 * b + 2 * t + 2)
                if j < 2:
                    pe.wait_ge(s_xm, 4 * (b + 1))
                r = R[(1, 2, 0, 1)[j]]
                if j == 3:
                    pe.wait_ge(s_XTs, 4 * b + 1)
                for c in range(4):
                    mm = pe.transpose(r[:, c * P:(c + 1) * P], HB[:, t, 4 * i + c, :], EYE[:, :])
                mm.then_inc(s_XT, 1)

            def hadamard(b, j):
                t, i = j // 2, j % 2
                pe.wait_ge(s_XTs, 4 * b + j + 1)
                pe.wait_ge(d_had, 16)
                r = R[(2, 0, 1, 2)[j]]
                if j == 0:
                    pe.wait_ge(s_XTs, 4 * b + 2)
                elif j == 1:
                    pe.wait_ge(s_XTs, 4 * b + 3)
                elif j == 2:
                    pe.wait_ge(s_XTs, 4 * b + 4)
                else:
                    pe.wait_ge(s_yq, 4 * b + 1)
                for p in range(2):
                    for e in range(2):
                        mm = pe.matmul(r[:, p * 2 * P:(p + 1) * 2 * P], XTS[:, t, 4 * i + 2 * p + e, :],
                                       HAD[:, e, :], start=(e == 0), stop=(e == 1))
                mm.then_inc(s_Y, 1)

            def turn_q2(b, t):
                pe.wait_ge(s_q2, 2 * b + t + 1)
                pe.wait_ge(s_yq, 4 * b + 2 * t + (2 if t == 0 else 1))
                r = R[t][:, :].bitcast(BF16)
                for c in range(G8):
                    mm = pe.transpose(r[:, c * P:(c + 1) * P], Q2[:, t, c * P:(c + 1) * P], EYEB[:, :])
                mm.then_inc(s_q2T, 1)

            def down(b, t):
                pe.wait_ge(s_q2Ts, 2 * b + t + 1)
                if t == 0:
                    pe.wait_ge(s_yq, 4 * b + 4)
                if b == 0:
                    pe.wait_ge(s_wter, 6)
                for c in range(G8):
                    mm = pe.matmul(R[2 if t == 0 else 0][:, 0:D], Q2T[:, t, c, :], WD[:, c, :],
                                   start=(c == 0), stop=(c == G8 - 1))
                mm.then_inc(s_dn, 1)

            def turn_x2(b):
                pe.wait_ge(s_xn2, 2 * (b + 1))
                pe.wait_ge(s_q2Ts, 2 * (b + 1))
                for c in range(T):
                    for t in range(T):
                        j = (c * T + t) * P
                        mm = pe.transpose(R[0][:, j:j + P], XN2[:, t, c * P:(c + 1) * P], EYE[:, :])
                mm.then_inc(s_x2T, 1)

            def attend(b):
                pe.wait_ge(s_x2Ts, b + 1)
                pe.wait_ge(s_AT, b + 1)
                for t in range(T):
                    for c in range(T):
                        mm = pe.matmul(R[1][:, t * D:(t + 1) * D], X2T[:, c, t, :], AT[:, b % 2, c, :],
                                       start=(c == 0), stop=(c == T - 1))
                mm.then_inc(s_pxm, 1)

            def turn_x3(b):
                pe.wait_ge(s_c3, b + 1)
                for c in range(T):
                    for t in range(T):
                        j = (c * T + t) * P
                        mm = pe.transpose(R[2][:, j:j + P], C3[:, t, c * P:(c + 1) * P], EYE[:, :])
                mm.then_inc(s_x3T, 1)

            def fc(b, j):
                t, i = j // 2, j % 2
                if j == 0:
                    pe.wait_ge(s_x3Ts, b + 1)
                    pe.wait_ge(s_x3, b + 1)
                    if b == 0:
                        pe.wait_ge(s_wter, 10)
                if j == 3:
                    pe.wait_ge(s_h, 4 * b + 1)
                for k in range(2):
                    mm = pe.matmul(R[j % 3][:, :], X3T[:, k, t, :], WFC[:, k, i * 512:(i + 1) * 512],
                                   start=(k == 0), stop=(k == 1))
                mm.then_inc(s_fc, 1)

            def turn_h(b, j):
                t, i = j // 2, j % 2
                pe.wait_ge(s_hc, 2 * b + t + 1)
                if j < 3:
                    pe.wait_ge(s_h, 4 * b + (2, 3, 4)[j])
                else:
                    pe.wait_ge(s_hTs, 4 * b + 1)
                for c in range(4):
                    mm = pe.transpose(R[(1, 2, 0, 1)[j]][:, c * P:(c + 1) * P],
                                      HC[:, t, (4 * i + c) * P:(4 * i + c + 1) * P], EYE[:, :])
                mm.then_inc(s_hT, 1)

            def project(b, t):
                pe.wait_ge(s_hTs, 4 * b + 2 * t + 2)
                for c in range(G8):
                    mm = pe.matmul(R[2 if t == 0 else 0][:, 0:D], HT[:, t, c, :], WPR[:, c, :],
                                   start=(c == 0), stop=(c == G8 - 1))
                mm.then_inc(s_pj, 1)

            prep_conv(0)
            prep_xdbl(0)
            prep_dt(0)
            pe.wait_ge(d_eye, 16)
            pe.wait_ge(s_eyeb, 1)
            for it in range(B + 2):
                b, nb, pb, tb = it, it + 1, it - 1, it - 2
                for k in range(SPOTS):
                    if b < B and k == 0:
                        bcast_b(b, 0)
                        bcast_c(b, 0)
                    if b < B and k % 6 == 2 and k // 6 + 1 < QUADS:
                        bcast_b(b, k // 6 + 1)
                    if b < B and k % 6 == 5 and k // 6 + 1 < QUADS:
                        bcast_c(b, k // 6 + 1)
                    if nb < B:
                        if k == 4:
                            prep_conv(nb)
                        if k == 6:
                            prep_xdbl(nb)
                        if k == 8:
                            prep_dt(nb)
                    if b < B:
                        if k == 13:
                            attn_qk(b)
                        if k == 15:
                            attn_energy(b)
                        if k == 20:
                            attn_turn(b)
                    if it == 0:
                        if k == 13:
                            weight_sums(0, 3)
                        if k == 19:
                            weight_sums(3, 2)
                    if 0 <= tb < B:
                        if k == 0:
                            turn_h(tb, 0)
                            turn_h(tb, 1)
                        if k == 1:
                            turn_h(tb, 2)
                            turn_h(tb, 3)
                        if k == 2:
                            project(tb, 0)
                        if k == 3:
                            project(tb, 1)
                    if 0 <= pb < B:
                        if k == 4:
                            turn_y(pb)
                        if k == 6:
                            turn_q1(pb)
                            gate_up(pb, 0)
                        if k in (8, 9, 10):
                            gate_up(pb, k - 7)
                        if k == 12:
                            turn_x(pb, 0)
                            turn_x(pb, 1)
                            hadamard(pb, 0)
                        if k == 14:
                            turn_x(pb, 2)
                            hadamard(pb, 1)
                            turn_x(pb, 3)
                            hadamard(pb, 2)
                        if k == 15:
                            hadamard(pb, 3)
                        if k == 17:
                            turn_q2(pb, 0)
                            down(pb, 0)
                        if k == 18:
                            turn_q2(pb, 1)
                            down(pb, 1)
                        if k == 20:
                            turn_x2(pb)
                            attend(pb)
                        if k == 22:
                            turn_x3(pb)
                            for j in range(4):
                                fc(pb, j)

        @block.scalar
        def _(act):
            def prep_act(b):
                act.wait_ge(s_conv, b + 1)
                act.wait_ge(d_vec, 48)
                act.wait_ge(s_wconv, 3)
                if b > 0:
                    act.wait_ge(s_w1e, 2 * b)
                for c in range(T):
                    act.activation(CACC[:, c, :], PA[:, c * L:(c + 1) * L], ACT.Identity,
                                   bias=VEC[:, 0, c:c + 1]).then_inc(s_act, 1)
                    act.activation(TH[:, c, :], PA[:, c * L:(c + 1) * L], ACT.Tanh,
                                   bias=HALF[:, 0, c:c + 1], scale=0.5).then_inc(s_act, 1)

            def prep_xd(b):
                act.wait_ge(s_xdbl, b + 1)
                if b > 0:
                    act.wait_ge(s_dtp, b)
                    act.wait_ge(s_parts, 4 * b)
                act.activation(XD[:, :], PA[0:104, 0:L], ACT.Copy, scale=0.5).then_inc(s_xd, 1)

            def prep_exp(b):
                act.wait_ge(s_dtp, b + 1)
                if b > 0:
                    act.wait_ge(s_w1e, 2 * b)
                for c in range(T):
                    act.activation(EB[:, c, :], PA[:, c * L:(c + 1) * L], ACT.Abs,
                                   bias=VEC[:, 1, c:c + 1]).then_inc(s_ax, 1)
                act.wait_ge(s_ax, 2 * (b + 1))
                act.activation(EB[:, :, :], EB[:, :, :], ACT.Exp, scale=-1.0).then_inc(s_e, 1)

            def prep_ln(b):
                act.wait_ge(s_w1e, 2 * b + 1)
                if b > 0:
                    act.wait_ge(s_dt, 2 * b)
                act.activation(LNB[:, :, :], WB[:, :, :], ACT.Ln).then_inc(s_ln, 1)

            def prep_z(b):
                act.wait_ge(s_zn, 2 * (b + 1))
                if b > 0:
                    act.wait_ge(s_sz, b)
                act.activation(ZTH[:, :, :], ZN[:, :, :], ACT.Tanh, scale=0.5).then_inc(s_zth, 1)

            def decay(b, s):
                g = STEPS * b + s
                q, c = s // T, s % T
                if s == 0:
                    act.wait_ge(s_dt, 2 * b + 1)
                    if b == 0:
                        act.wait_ge(s_aneg, 1)
                        act.wait_ge(s_const, 4)
                if g >= NDA:
                    act.wait_ge(s_scan, g - NDA + 1)
                for n in range(NQ):
                    i = act.activation(DA[:, g % NDA, n, 1:L], DT[:, b % 2, c, 1:L], ACT.Exp,
                                       scale=ANEG[:, c, NQ * q + n:NQ * q + n + 1])
                i.then_inc(s_da, 1)

            def attn_qk(b):
                act.wait_ge(s_pqk, b + 1)
                if b > 0:
                    act.wait_ge(s_en, b)
                for i in range(2):
                    act.activation(QK[:, i, :], PA[:, i * L:(i + 1) * L], ACT.Identity,
                                   bias=BQK[:, i:i + 1]).then_inc(s_qk, 1)

            def attn_exp(b):
                act.wait_ge(s_mx, b + 1)
                if b > 0:
                    act.wait_ge(s_pn, 2 * b)
                for t in range(T):
                    act.activation(EX[:, t, :], PA[:, t * L:(t + 1) * L], ACT.Exp, bias=NMX[:, t:t + 1],
                                   accum_out=RSUM[:, t:t + 1]).then_inc(s_ex, 1)

            def attn_copy(b):
                act.wait_ge(s_pT, b + 1)
                if b > 1:
                    act.wait_ge(s_pxm, b - 1)
                act.activation(AT[:, b % 2, :, :], PA[:, :].rearrange("p (c l) -> p c l", c=T),
                               ACT.Copy).then_inc(s_AT, 1)

            def weight_src(i):
                return (WRAW[0], WRAW[1], WRAW[2],
                        WFC[:, :, :].rearrange("p k f -> p (k f)"),
                        WPR[:, :, :].rearrange("p k f -> p (k f)"))[i]

            def weight_abs(i):
                act.wait_ge(d_w[i], 16)
                if i:
                    act.wait_ge(s_wabs, i)
                act.activation(WABS, weight_src(i), ACT.Abs,
                               accum_out=WSUM[:, i:i + 1]).then_inc(s_wabs, 1)

            def weight_round(i):
                act.wait_ge(s_wsc, 5 if i < 3 else 10)
                act.activation(weight_src(i), weight_src(i), ACT.Identity, bias=ROUNDC[:, 0:1],
                               scale=WREC[:, i:i + 1]).then_inc(s_wrnd, 1)

            def copy_q1(b):
                act.wait_ge(s_qT, b + 1)
                if b > 0:
                    act.wait_ge(s_gu, 4 * b)
                act.activation(QT[:, :, :, :].rearrange("p a b c -> p (a b c)"),
                               R[1][:, 0:256].bitcast(BF16), ACT.Copy).then_inc(s_qTs, 1)

            def gate_tanh(b, j):
                act.wait_ge(s_gu, 4 * b + j + 1)
                act.wait_ge(s_am, 7 * (b + 1))
                if 4 * b + j >= 2:
                    act.wait_ge(s_sg, 4 * b + j - 1)
                act.activation(TG[:, j % 2, :], R[(2 * j + 2) % 3][:, :], ACT.Tanh,
                               scale=GAH[:, j // 2:j // 2 + 1]).then_inc(s_tg, 1)

            def copy_x(b, j):
                t, i = j // 2, j % 2
                act.wait_ge(s_XT, 4 * b + j + 1)
                if b > 0:
                    act.wait_ge(s_Y, 4 * b)
                act.activation(XTS[:, t, 4 * i:4 * i + 4, :], R[(1, 2, 0, 1)[j]][:, :].rearrange(
                    "p (c l) -> p c l", c=4), ACT.Copy).then_inc(s_XTs, 1)

            def quant_y(b, j):
                t, i = j // 2, j % 2
                act.wait_ge(s_qs2, 10 * b + 5 * t + 5)
                if b > 0:
                    act.wait_ge(s_q2, 2 * b)
                act.activation(YQ[:, t, i * 512:(i + 1) * 512], R[(2, 0, 1, 2)[j]][:, :], ACT.Identity,
                               bias=ROUNDC[:, 0:1], scale=QS2[:, t:t + 1]).then_inc(s_yq, 1)

            def copy_q2(b, t):
                act.wait_ge(s_q2T, 2 * b + t + 1)
                if b > 0:
                    act.wait_ge(s_dn, 2 * b)
                act.activation(Q2T[:, t, :, :].rearrange("p c l -> p (c l)"), R[t][:, :].bitcast(BF16),
                               ACT.Copy).then_inc(s_q2Ts, 1)

            def copy_x2(b):
                act.wait_ge(s_x2T, b + 1)
                if b > 0:
                    act.wait_ge(s_pxm, b)
                act.activation(X2T[:, :, :, :].rearrange("p a b c -> p (a b c)"), R[0][:, :],
                               ACT.Copy).then_inc(s_x2Ts, 1)

            def copy_x3(b):
                act.wait_ge(s_x3T, b + 1)
                if b > 0:
                    act.wait_ge(s_fc, 4 * b)
                act.activation(X3T[:, :, :, :].rearrange("p a b c -> p (a b c)"), R[2][:, :],
                               ACT.Copy).then_inc(s_x3Ts, 1)

            def gelu(b, j):
                t, i = j // 2, j % 2
                act.wait_ge(s_fc, 4 * b + j + 1)
                if b > 0:
                    act.wait_ge(s_hd, 2 * b)
                act.activation(HG[:, t, i * 512:(i + 1) * 512], R[j % 3][:, :], ACT.Gelu,
                               scale=S1[:, t:t + 1]).then_inc(s_h, 1)

            def copy_h(b, j):
                t, i = j // 2, j % 2
                act.wait_ge(s_hT, 4 * b + j + 1)
                if b > 0:
                    act.wait_ge(s_pj, 2 * b)
                act.activation(HT[:, t, 4 * i:4 * i + 4, :], R[(1, 2, 0, 1)[j]][:, :].rearrange(
                    "p (c l) -> p c l", c=4), ACT.Copy).then_inc(s_hTs, 1)

            act.wait_ge(d_alog, 16)
            prep_act(0)
            prep_xd(0)
            prep_exp(0)
            act.activation(AEXP[:, :, :], ALOG[:, :, :], ACT.Exp).then_inc(s_aexp, 1)
            prep_ln(0)
            prep_z(0)
            act.wait_ge(s_const, 4)
            for it in range(B + 2):
                b, nb, pb, tb = it, it + 1, it - 1, it - 2
                if b < B:
                    decay(b, 0)
                    decay(b, 1)
                for k in range(SPOTS):
                    if b < B and k % 3 == 0 and k // 3 + 2 < STEPS:
                        decay(b, k // 3 + 2)
                    if nb < B:
                        if k == 4:
                            prep_act(nb)
                        if k == 6:
                            prep_xd(nb)
                        if k == 8:
                            prep_exp(nb)
                        if k == 10:
                            prep_ln(nb)
                        if k == 17:
                            prep_z(nb)
                    if b < B:
                        if k == 13:
                            attn_qk(b)
                        if k == 17:
                            attn_exp(b)
                        if k == 21:
                            attn_copy(b)
                    if it == 0:
                        if k in (8, 9, 10):
                            weight_abs(k - 8)
                        if k in (15, 16):
                            weight_abs(k - 12)
                        if k in (17, 18, 19):
                            weight_round(k - 17)
                        if k in (21, 22):
                            weight_round(k - 18)
                    if 0 <= tb < B:
                        if k == 0:
                            copy_h(tb, 0)
                            copy_h(tb, 1)
                        if k == 1:
                            copy_h(tb, 2)
                            copy_h(tb, 3)
                    if 0 <= pb < B:
                        if k == 6:
                            copy_q1(pb)
                            gate_tanh(pb, 0)
                        if k in (8, 9, 10):
                            gate_tanh(pb, k - 7)
                        if k == 12:
                            copy_x(pb, 0)
                            copy_x(pb, 1)
                        if k == 14:
                            copy_x(pb, 2)
                            copy_x(pb, 3)
                        if k == 15:
                            quant_y(pb, 0)
                            quant_y(pb, 1)
                        if k == 16:
                            quant_y(pb, 2)
                            quant_y(pb, 3)
                        if k == 17:
                            copy_q2(pb, 0)
                        if k == 18:
                            copy_q2(pb, 1)
                        if k == 20:
                            copy_x2(pb)
                        if k == 22:
                            copy_x3(pb)
                        if k == 23:
                            for j in range(4):
                                gelu(pb, j)

        @block.vector
        def _(dve):
            def norm_stats(i, b, src, scale, add):
                for t in range(T):
                    dve.bn_stats(STT[:, i, t, :], src[:, t, :]).then_inc(s_lnst[i], 1)
                for t in range(T):
                    dve.wait_ge(s_lnst[i], 5 * b + t + 1)
                    dve.bn_aggr(MV[:, i, t, :], STT[:, i, t, :]).then_inc(s_lnst[i], 1)
                dve.wait_ge(s_lnst[i], 5 * b + 4)
                dve.tensor_scalar(VE[:, i, :], MV[:, i, :, 1], scale, add, ALU.mult, ALU.add)\
                    .then_inc(s_lnst[i], 1)

            def norm_rows(i, b, src, dst, done):
                dve.wait_ge(s_rstd[i], b + 1)
                for t in range(T):
                    dve.tensor_scalar(dst[:, t, :], src[:, t, :], MV[:, i, t, 0:1], RS[:, i, t:t + 1],
                                      ALU.subtract, ALU.mult).then_inc(done, 1)

            def prep_u(b):
                dve.wait_ge(s_act, 4 * (b + 1))
                if b > 1:
                    dve.wait_ge(s_v, 3 * (b - 1))
                dve.scalar_tensor_tensor(out=U2[:, b % 2, :, :], in0=TH[:, :, :], scalar=1.0,
                                         in1=CACC[:, :, :], op0=ALU.add, op1=ALU.mult).then_inc(s_u, 1)

            def prep_split(b):
                pt = PARTS[:, b % 2, :]
                dve.wait_ge(s_xd, b + 1)
                if b > 1:
                    dve.wait_ge(s_cb, QUADS * (b - 1))
                dve.tensor_copy(pt, XD[0:96, :]).then_inc(s_parts, 1)
                dve.wait_ge(s_parts, 4 * b + 1)
                dve.tensor_tensor(R1, XD[0:96, :], pt, ALU.subtract).then_inc(s_parts, 1)
                dve.wait_ge(s_parts, 4 * b + 2)
                dve.tensor_copy(pt[32:64, :], R1[32:64, :])
                dve.tensor_copy(pt[64:96, :], R1[64:96, :]).then_inc(s_parts, 1)
                dve.wait_ge(s_parts, 4 * b + 3)
                dve.tensor_tensor(pt[64:96, :], R1[64:96, :], pt[64:96, :], ALU.subtract).then_inc(s_parts, 1)

            def prep_softplus1(b):
                dve.wait_ge(s_ax, 2 * (b + 1))
                for c in range(T):
                    dve.tensor_scalar(RELU[:, c, :], PA[:, c * L:(c + 1) * L], VEC[:, 1, c:c + 1], 0.0,
                                      ALU.add, ALU.max).then_inc(s_relu, 1)
                dve.wait_ge(s_e, b + 1)
                dve.tensor_scalar(WB[:, :, :], EB[:, :, :], 1.0, None, ALU.add).then_inc(s_w1e, 1)
                dve.wait_ge(s_w1e, 2 * b + 1)
                dve.scalar_tensor_tensor(out=RES[:, :, :], in0=WB[:, :, :], scalar=-1.0, in1=EB[:, :, :],
                                         op0=ALU.add, op1=ALU.subtract).then_inc(s_w1e, 1)
                dve.wait_ge(s_w1e, 2 * b + 2)
                dve.wait_ge(s_relu, 2 * b + 2)
                dve.tensor_tensor(RELU[:, :, :], RELU[:, :, :], RES[:, :, :], ALU.subtract).then_inc(s_res, 1)

            def prep_softplus2(b):
                dve.wait_ge(s_ln, b + 1)
                dve.wait_ge(s_res, b + 1)
                if b > 1:
                    dve.wait_ge(s_da, STEPS * (b - 1))
                dve.tensor_tensor(DT[:, b % 2, :, :], LNB[:, :, :], RELU[:, :, :], ALU.add).then_inc(s_dt, 1)
                dve.wait_ge(s_dt, 2 * b + 1)
                dve.scalar_tensor_tensor(out=DTU[:, b % 2, :, :], in0=DT[:, b % 2, :, :], scalar=0.5,
                                         in1=U2[:, b % 2, :, :], op0=ALU.mult, op1=ALU.mult).then_inc(s_dt, 1)

            def prep_sz(b):
                dve.wait_ge(s_zth, b + 1)
                dve.scalar_tensor_tensor(out=SZ[:, b % 2, :, :], in0=ZTH[:, :, :], scalar=1.0,
                                         in1=ZN[:, :, :], op0=ALU.add, op1=ALU.mult).then_inc(s_sz, 1)

            def drive(b, s):
                g, q, c = STEPS * b + s, s // T, s % T
                dve.wait_ge(s_dt, 2 * (b + 1))
                dve.wait_ge(s_bb, QUADS * b + q + 1)
                if g >= NH:
                    dve.wait_ge(s_z, g - NH + 1)
                dve.tensor_tensor(H[:, g % NH, :, :], BB[:, :, :],
                                  DTU[:, b % 2, c, :].unsqueeze(1).to_broadcast([P, NQ, L]),
                                  ALU.mult).then_inc(s_dbu, 1)

            def scan(b, s):
                g = STEPS * b + s
                dve.wait_ge(s_da, g + 1)
                dve.wait_ge(s_dbu, g + 1)
                hh = H[:, g % NH, :, :].rearrange("p n l -> p (n l)")
                dve.tensor_tensor_scan(hh, DA[:, g % NDA, :, :].rearrange("p n l -> p (n l)"), hh, 0.0,
                                       ALU.mult, ALU.add).then_inc(s_scan, 1)

            def read_out(b, s):
                g, q = STEPS * b + s, s // T
                dve.wait_ge(s_scan, g + 1)
                dve.wait_ge(s_cb, QUADS * b + q + 1)
                if g >= NZ:
                    ob, os = (g - NZ) // STEPS, (g - NZ) % STEPS
                    dve.wait_ge(s_acc, 6 * ob + (max(os - 1, 1) if os >= 2 else os + 1))
                dve.tensor_tensor(Z[:, g % NZ, :, :], CB[:, :, :], H[:, g % NH, :, :], ALU.mult)\
                    .then_inc(s_z, 1)

            def attn_max(b):
                dve.wait_ge(s_en, b + 1)
                if b > 0:
                    dve.wait_ge(s_ex, 2 * b)
                dve.tensor_reduce(NMX[:, :], PA[:, :].rearrange("p (t l) -> p t l", t=T), AX.X, ALU.max,
                                  negate=True).then_inc(s_mx, 1)

            def attn_norm(b):
                dve.wait_ge(s_ex, 2 * (b + 1))
                dve.reciprocal(RINV[:, :], RSUM[:, :]).then_inc(s_rinv, 1)
                dve.wait_ge(s_rinv, b + 1)
                if b > 0:
                    dve.wait_ge(s_pT, b)
                for t in range(T):
                    dve.tensor_scalar(PN[:, t, :], EX[:, t, :], RINV[:, t:t + 1], None, ALU.mult)\
                        .then_inc(s_pn, 1)

            def weight_scales(first, n):
                dve.wait_ge(s_wtot, 1 if first == 0 else 2)
                cols = slice(first, first + n)
                w = 5 if first else 0
                if first == 0:
                    dve.tensor_scalar(WMEAN[:, cols], R[0][:, 0:n], 1.0 / (FF * D), EPS0, ALU.mult, ALU.max)\
                        .then_inc(s_wsc, 1)
                    dve.wait_ge(s_wsc, 1)
                    dve.reciprocal(WREC[:, cols], WMEAN[:, cols]).then_inc(s_wsc, 1)
                    dve.tensor_scalar(WSC[:, 0:1], WMEAN[:, 0:1], 1.0 / (2 * QB), None, ALU.mult)\
                        .then_inc(s_wsc, 1)
                    dve.scalar_tensor_tensor(out=WSC[:, 1:2], in0=WMEAN[:, 0:1], scalar=1.0 / (64 * QB * QB),
                                             in1=WMEAN[:, 1:2], op0=ALU.mult, op1=ALU.mult).then_inc(s_wsc, 1)
                    dve.tensor_scalar(WSC[:, 2:3], WMEAN[:, 2:3], 1.0 / QB, None, ALU.mult).then_inc(s_wsc, 1)
                else:
                    dve.tensor_scalar(WMEAN[:, cols], R[0][:, 0:n], 1.0 / (FF * D), None, ALU.mult)\
                        .then_inc(s_wsc, 1)
                    dve.wait_ge(s_wsc, w + 1)
                    dve.tensor_scalar(WDIV[:, cols], WMEAN[:, cols], EPS1, None, ALU.add).then_inc(s_wsc, 1)
                    dve.wait_ge(s_wsc, w + 2)
                    dve.reciprocal(WREC[:, cols], WDIV[:, cols]).then_inc(s_wsc, 3)

            def weight_ternary(i):
                src = (WRAW[0], WRAW[1], WRAW[2],
                       WFC[:, :, :].rearrange("p k f -> p (k f)"), WPR[:, :, :].rearrange("p k f -> p (k f)"))[i]
                dst = (WG, WU, WD, WFC, WPR)[i][:, :, :].rearrange("p k f -> p (k f)")
                dve.wait_ge(s_wrnd, i + 1)
                dve.tensor_scalar(dst, src, ROUND, 1.0, ALU.subtract, ALU.min).then_inc(s_wter, 1)
                dve.wait_ge(s_wter, 2 * i + 1)
                dve.tensor_scalar(dst, dst, -1.0, None, ALU.max).then_inc(s_wter, 1)

            def gate_y(b):
                dve.wait_ge(s_fold, 4 * (b + 1))
                if b > 0:
                    dve.wait_ge(s_yT, b)
                for c in range(T):
                    dve.scalar_tensor_tensor(out=YS[:, c, :], in0=U2[:, b % 2, c, :], scalar=HALF[:, 1, c:c + 1],
                                             in1=YS[:, c, :], op0=ALU.mult, op1=ALU.add).then_inc(s_v, 1)
                dve.wait_ge(s_v, 3 * b + 2)
                dve.wait_ge(s_sz, b + 1)
                dve.tensor_tensor(V2[:, :, :], YS[:, :, :], SZ[:, b % 2, :, :], ALU.mult).then_inc(s_v, 1)

            def rows_x1(b):
                dve.wait_ge(s_yT, b + 1)
                dve.scalar_tensor_tensor(out=X1[:, :, :], in0=R[0][:, :].rearrange("p (t d) -> p t d", t=T),
                                         scalar=0.5, in1=X[:, b, :, :], op0=ALU.mult, op1=ALU.add)\
                    .then_inc(s_x1, 1)
                dve.wait_ge(s_x1, b + 1)
                norm_stats(1, b, X1, 1.0, EPS0)

            def quant1(b):
                norm_rows(1, b, X1, XN, s_xn)
                dve.wait_ge(s_xn, 2 * (b + 1))
                a = 7 * b
                if b > 0:
                    dve.wait_ge(s_tg, 4 * b)
                dve.tensor_reduce(AM[:, :], XN[:, :, :], AX.X, ALU.max, apply_absolute_value=True)\
                    .then_inc(s_am, 1)
                dve.wait_ge(s_am, a + 1)
                dve.tensor_scalar(AMC[:, :], AM[:, :], EPS0, None, ALU.max).then_inc(s_am, 1)
                dve.wait_ge(s_am, a + 2)
                dve.reciprocal(RC[:, :], AMC[:, :]).then_inc(s_am, 1)
                dve.tensor_scalar(GAH[:, :], AMC[:, :], WSC[:, 0:1], None, ALU.mult).then_inc(s_am, 1)
                dve.tensor_scalar(KA[:, :], AMC[:, :], WSC[:, 1:2], None, ALU.mult).then_inc(s_am, 1)
                dve.wait_ge(s_am, a + 5)
                dve.tensor_scalar(QS[:, :], RC[:, :], QB, None, ALU.mult).then_inc(s_am, 1)
                dve.tensor_tensor(KK[:, :], KA[:, :], AMC[:, :], ALU.mult).then_inc(s_am, 1)
                dve.wait_ge(s_am, a + 6)
                for t in range(T):
                    dve.tensor_scalar(XQ[:, t, :], XN[:, t, :], QS[:, t:t + 1], QB - 1, ALU.mult, ALU.min)\
                        .then_inc(s_q1, 1)
                dve.wait_ge(s_q1, 3 * b + 2)
                if b > 0:
                    dve.wait_ge(s_qT, b)
                dve.tensor_scalar(Q1[:, :, :], XQ[:, :, :], ROUND, ROUND, ALU.add, ALU.subtract)\
                    .then_inc(s_q1, 1)

            def gated(b, j):
                t, i = j // 2, j % 2
                n = 4 * b + j
                dve.wait_ge(s_tg, n + 1)
                dve.scalar_tensor_tensor(out=SG[:, j % 2, :], in0=TG[:, j % 2, :], scalar=1.0,
                                         in1=R[(2 * j + 2) % 3][:, :], op0=ALU.add, op1=ALU.mult)\
                    .then_inc(s_sg, 1)
                dve.wait_ge(s_sg, n + 1)
                if b > 0:
                    dve.wait_ge(s_hA, 4 * b)
                dve.tensor_tensor(XM[:, t, 4 * i:4 * i + 4, :], SG[:, j % 2, :].rearrange("p (c l) -> p c l", c=4),
                                  R[(2 * j + 3) % 3][:, :].rearrange("p (c l) -> p c l", c=4), ALU.mult)\
                    .then_inc(s_xm, 1)

            def stage_b(b, t):
                dve.wait_ge(s_hA, 4 * b + 2 * t + 2)
                if b > 0:
                    dve.wait_ge(s_XT, 4 * b)
                a = HA[:, t, :, :].rearrange("p (a b e) l -> p a b (e l)", a=2, b=2)
                o = HB[:, t, :, :].rearrange("p (a b e) l -> p a b (e l)", a=2, b=2)
                dve.tensor_tensor(o[:, :, 0, :], a[:, :, 0, :], a[:, :, 1, :], ALU.add).then_inc(s_hB, 1)
                dve.tensor_tensor(o[:, :, 1, :], a[:, :, 0, :], a[:, :, 1, :], ALU.subtract).then_inc(s_hB, 1)

            def scales2(b, t):
                n = 10 * b + 5 * t
                for i in range(2):
                    j = 2 * t + i
                    dve.wait_ge(s_Y, 4 * b + j + 1)
                    dve.tensor_reduce(AM2[:, t, i:i + 1], R[(2, 0, 1, 2)[j]][:, :], AX.X, ALU.max,
                                      apply_absolute_value=True).then_inc(s_am2, 1)
                dve.wait_ge(s_am2, 4 * b + 2 * t + 2)
                if b > 0:
                    dve.wait_ge(s_x2, 2 * b)
                dve.tensor_tensor(AMX[:, t:t + 1], AM2[:, t, 0:1], AM2[:, t, 1:2], ALU.max).then_inc(s_qs2, 1)
                dve.wait_ge(s_qs2, n + 1)
                dve.tensor_scalar(AMT[:, t:t + 1], AMX[:, t:t + 1], KK[:, t:t + 1], EPS0, ALU.mult, ALU.max)\
                    .then_inc(s_qs2, 1)
                dve.wait_ge(s_qs2, n + 2)
                dve.reciprocal(RC2[:, t:t + 1], AMT[:, t:t + 1]).then_inc(s_qs2, 1)
                dve.tensor_scalar(DSC[:, t:t + 1], AMT[:, t:t + 1], WSC[:, 2:3], None, ALU.mult)\
                    .then_inc(s_qs2, 1)
                dve.wait_ge(s_qs2, n + 4)
                dve.tensor_scalar(QS2[:, t:t + 1], RC2[:, t:t + 1], KK[:, t:t + 1], QB, ALU.mult, ALU.mult)\
                    .then_inc(s_qs2, 1)

            def quant2(b, t):
                dve.wait_ge(s_yq, 4 * b + 2 * t + 2)
                if b > 0:
                    dve.wait_ge(s_q2T, 2 * b)
                dve.tensor_scalar(Q2[:, t, :], YQ[:, t, :], ROUND, QB - 1, ALU.subtract, ALU.min)\
                    .then_inc(s_q2, 1)

            def rows_x2(b):
                for t in range(T):
                    dve.wait_ge(s_dn, 2 * b + t + 1)
                    dve.scalar_tensor_tensor(out=X2[:, t, :], in0=R[2 if t == 0 else 0][:, 0:D],
                                             scalar=DSC[:, t:t + 1], in1=X1[:, t, :], op0=ALU.mult,
                                             op1=ALU.add).then_inc(s_x2, 1)
                dve.wait_ge(s_x2, 2 * (b + 1))
                norm_stats(2, b, X2, 1.0, EPS0)

            def rows_x3(b):
                dve.wait_ge(s_pxm, b + 1)
                dve.tensor_tensor(X3[:, :, :], R[1][:, :].rearrange("p (t d) -> p t d", t=T), X2[:, :, :],
                                  ALU.add).then_inc(s_x3, 1)
                dve.wait_ge(s_x3, b + 1)
                norm_stats(3, b, X3, 1.0 + EPS1, EPS0 * EPS1)

            def scales3(b):
                norm_rows(3, b, X3, D3, s_d3)
                a = 5 * b
                dve.wait_ge(s_d3, 2 * (b + 1))
                if b > 0:
                    dve.wait_ge(s_c3, b)
                    dve.wait_ge(s_h, 4 * b)
                dve.tensor_reduce(GM[:, :], D3[:, :, :], AX.X, ALU.max, apply_absolute_value=True)\
                    .then_inc(s_gm, 1)
                dve.wait_ge(s_gm, a + 1)
                dve.reciprocal(GI[:, :], GM[:, :]).then_inc(s_gm, 1)
                dve.tensor_scalar(NG[:, :], GM[:, :], -1.0, None, ALU.mult).then_inc(s_gm, 1)
                dve.wait_ge(s_gm, a + 3)
                dve.tensor_tensor(GN[:, :], GM[:, :], GI[:, :], ALU.mult).then_inc(s_gm, 1)
                dve.wait_ge(s_gm, a + 4)
                dve.tensor_scalar(S1[:, :], GN[:, :], WMEAN[:, 3:4], None, ALU.mult).then_inc(s_gm, 1)
                for t in range(T):
                    i = dve.tensor_scalar(C3[:, t, :], D3[:, t, :], GM[:, t:t + 1], NG[:, t:t + 1],
                                          ALU.min, ALU.max)
                i.then_inc(s_c3, 1)

            def hidden_stats(b, j):
                t, i = j // 2, j % 2
                dve.wait_ge(s_h, 4 * b + j + 1)
                dve.bn_stats(ST3[:, t, i, :], HG[:, t, i * 512:(i + 1) * 512]).then_inc(s_st3, 1)

            def hidden_norm(b, t):
                dve.wait_ge(s_st3, 8 * b + 4 + 2 * t)
                dve.bn_aggr(MV3[:, t, :], ST3[:, t, :, :].rearrange("p a b -> p (a b)")).then_inc(s_st3, 1)
                dve.wait_ge(s_st3, 8 * b + 5 + 2 * t)
                dve.tensor_scalar(VE3[:, t:t + 1], MV3[:, t, 1:2], EPS1, None, ALU.add).then_inc(s_st3, 1)

            def hidden_range(b, t):
                n = 10 * b + 5 * t
                dve.wait_ge(s_hd, 2 * b + t + 1)
                dve.tensor_reduce(GM2[:, t:t + 1], HD[:, t, :], AX.X, ALU.max, apply_absolute_value=True)\
                    .then_inc(s_gm2, 1)
                dve.wait_ge(s_gm2, n + 1)
                dve.tensor_scalar(NG2[:, t:t + 1], GM2[:, t:t + 1], -1.0, None, ALU.mult).then_inc(s_gm2, 1)
                dve.reciprocal(GI2[:, t:t + 1], GM2[:, t:t + 1]).then_inc(s_gm2, 1)
                dve.wait_ge(s_gm2, n + 3)
                dve.tensor_tensor(GN2[:, t:t + 1], GM2[:, t:t + 1], GI2[:, t:t + 1], ALU.mult).then_inc(s_gm2, 1)
                dve.wait_ge(s_gm2, n + 4)
                dve.tensor_scalar(S2[:, t:t + 1], GN2[:, t:t + 1], WMEAN[:, 4:5], None, ALU.mult)\
                    .then_inc(s_gm2, 1)

            def rows_out(b, t):
                dve.wait_ge(s_pj, 2 * b + t + 1)
                dve.wait_ge(s_gm2, 10 * b + 5 * t + 5)
                if b > 1:
                    dve.wait_ge(d_out[b - 2], 16 * T)
                dve.scalar_tensor_tensor(out=XO[:, b % 2, t, :], in0=R[2 if t == 0 else 0][:, 0:D],
                                         scalar=S2[:, t:t + 1], in1=X3[:, t, :], op0=ALU.mult,
                                         op1=ALU.add).then_inc(s_o, 1)

            dve.memset(CT[:, :, 0:TAPS - 1], 0.0).then_inc(s_const, 1)
            dve.memset(ONES[:, :], 1.0).then_inc(s_const, 1)
            dve.memset(ROUNDC[:, :], ROUND).then_inc(s_const, 1)
            dve.memset(DA[:, :, :, 0], 0.0).then_inc(s_const, 1)
            dve.wait_ge(d_in, 16)
            dve.wait_ge(d_cw, 16)
            dve.tensor_tensor(WCONV[:, :, :], CW, INW[:, :].unsqueeze(1).to_broadcast([P, TAPS, D]),
                              ALU.mult).then_inc(s_wconv, 1)
            dve.wait_ge(d_vec, 48)
            dve.tensor_scalar(HALF[:, 0, :], VEC[:, 0, :], 0.5, None, ALU.mult).then_inc(s_wconv, 1)
            dve.tensor_scalar(HALF[:, 1, :], VEC[:, 2, :], 0.5, None, ALU.mult).then_inc(s_wconv, 1)
            dve.wait_ge(d_x[0], 16)
            norm_stats(0, 0, X[:, 0, :, :], 1.0, EPS0)
            prep_u(0)
            prep_split(0)
            norm_rows(0, 0, X[:, 0, :, :], ZN, s_zn)
            dve.wait_ge(d_sel, 16)
            dve.tensor_copy(SEL[:, :, :], SELC[:, :].unsqueeze(2).to_broadcast([96, 32, P])).then_inc(s_sel, 1)
            prep_softplus1(0)
            dve.wait_ge(s_aexp, 1)
            dve.tensor_scalar(ANEG[:, :, :], AEXP[:, :, :], -1.0, None, ALU.mult).then_inc(s_aneg, 1)
            prep_softplus2(0)
            prep_sz(0)
            dve.wait_ge(d_eye, 16)
            dve.tensor_copy(EYEB[:, :], EYE[:, :]).then_inc(s_eyeb, 1)
            for it in range(B + 2):
                b, nb, pb, tb = it, it + 1, it - 1, it - 2
                for k in range(SPOTS):
                    if b < B:
                        s = 2 * (k // 6) + k % 2
                        (drive, scan, read_out)[k % 6 // 2](b, s)
                    if nb < B:
                        if k == 6:
                            prep_u(nb)
                        if k == 8:
                            prep_split(nb)
                        if k == 10:
                            prep_softplus1(nb)
                        if k == 12:
                            prep_softplus2(nb)
                        if k == 11:
                            dve.wait_ge(d_x[nb], 16)
                            norm_stats(0, nb, X[:, nb, :, :], 1.0, EPS0)
                        if k == 16:
                            norm_rows(0, nb, X[:, nb, :, :], ZN, s_zn)
                        if k == 19:
                            prep_sz(nb)
                    if b < B:
                        if k == 16:
                            attn_max(b)
                        if k == 19:
                            attn_norm(b)
                    if it == 0:
                        if k == 14:
                            weight_scales(0, 3)
                        if k == 20:
                            weight_scales(3, 2)
                        if k in (18, 19, 20):
                            weight_ternary(k - 18)
                        if k in (22, 23):
                            weight_ternary(k - 19)
                    if 0 <= tb < B:
                        if k == 2:
                            rows_out(tb, 0)
                        if k == 3:
                            rows_out(tb, 1)
                    if 0 <= pb < B:
                        if k == 4:
                            gate_y(pb)
                        if k == 5:
                            rows_x1(pb)
                        if k == 6:
                            quant1(pb)
                        if k in (8, 9, 10, 11):
                            gated(pb, k - 8)
                        if k == 12:
                            stage_b(pb, 0)
                        if k == 14:
                            stage_b(pb, 1)
                        if k in (15, 16):
                            scales2(pb, k - 15)
                        if k in (17, 18):
                            quant2(pb, k - 17)
                        if k == 19:
                            rows_x2(pb)
                        if k == 20:
                            norm_rows(2, pb, X2, XN2, s_xn2)
                        if k == 21:
                            rows_x3(pb)
                        if k == 22:
                            scales3(pb)
                        if k == 23:
                            for j in range(4):
                                hidden_stats(pb, j)
                            hidden_norm(pb, 0)
                            hidden_norm(pb, 1)
                            hidden_range(pb, 0)
                            hidden_range(pb, 1)

        @block.gpsimd
        def _(pool):
            def inverse_root(i, b):
                pool.wait_ge(s_lnst[i], 5 * (b + 1))
                pool.tensor_tensor(RS[:, i, :], VE[:, i, :], MHALF[:, 0:T], ALU.pow).then_inc(s_rstd[i], 1)

            def sum_step(b, s):
                g, q, c = STEPS * b + s, s // T, s % T
                pool.wait_ge(s_z, g + 1)
                if q == 1:
                    if b > 0:
                        pool.wait_ge(s_fold, 4 * (b - 1) + 2 * c + 1)
                    pool.tensor_tensor(ACC[:, c, :, :], Z[:, (g - T) % NZ, :, :], Z[:, g % NZ, :, :],
                                       ALU.add).then_inc(s_acc, 1)
                else:
                    pool.wait_ge(s_acc, 6 * b + s - 3)
                    pool.tensor_tensor(ACC[:, c, :, :], ACC[:, c, :, :], Z[:, g % NZ, :, :],
                                       ALU.add).then_inc(s_acc, 1)

            def fold(b, c):
                pool.wait_ge(s_acc, 6 * b + 5 + c)
                pool.tensor_tensor(FOLD[:, c, :, :], ACC[:, c, 0:2, :], ACC[:, c, 2:4, :], ALU.add)\
                    .then_inc(s_fold, 1)
                pool.wait_ge(s_fold, 4 * b + 2 * c + 1)
                if b > 0:
                    pool.wait_ge(s_v, 3 * b)
                pool.tensor_tensor(YS[:, c, :], FOLD[:, c, 0, :], FOLD[:, c, 1, :], ALU.add).then_inc(s_fold, 1)

            def stage_a(b, t):
                pool.wait_ge(s_xm, 4 * b + 2 * t + 2)
                if b > 0:
                    pool.wait_ge(s_hB, 4 * b)
                for i, op in enumerate((ALU.add, ALU.subtract)):
                    pool.tensor_tensor(HA[:, t, 4 * i:4 * i + 4, :], XM[:, t, 0:4, :], XM[:, t, 4:8, :], op)\
                        .then_inc(s_hA, 1)

            def hidden_rows(b, t):
                pool.wait_ge(s_st3, 8 * b + 6 + 2 * t)
                pool.tensor_tensor(RS3[:, t:t + 1], VE3[:, t:t + 1], MHALF[:, 0:1], ALU.pow).then_inc(s_rs3, 1)
                pool.wait_ge(s_rs3, 2 * b + t + 1)
                if b > 0:
                    pool.wait_ge(s_hc, 2 * b)
                pool.tensor_scalar(HD[:, t, :], HG[:, t, :], MV3[:, t, 0:1], RS3[:, t:t + 1],
                                   ALU.subtract, ALU.mult).then_inc(s_hd, 1)

            def hidden_clip(b, t):
                pool.wait_ge(s_gm2, 10 * b + 5 * t + 2)
                if b > 0:
                    pool.wait_ge(s_hT, 4 * b)
                pool.tensor_scalar(HC[:, t, :], HD[:, t, :], GM2[:, t:t + 1], NG2[:, t:t + 1],
                                   ALU.min, ALU.max).then_inc(s_hc, 1)

            pool.memset(MHALF[:, :], -0.5).then_inc(s_mhalf, 1)
            pool.wait_ge(s_mhalf, 1)
            inverse_root(0, 0)
            for it in range(B + 2):
                b, nb, pb, tb = it, it + 1, it - 1, it - 2
                for k in range(SPOTS):
                    if b < B:
                        s = 2 * (k // 6) + k % 2
                        if k % 6 // 2 == 2 and s >= T:
                            sum_step(b, s)
                    if k == 11 and nb < B:
                        inverse_root(0, nb)
                    if 0 <= tb < B:
                        if k == 0:
                            hidden_clip(tb, 0)
                            hidden_clip(tb, 1)
                    if 0 <= pb < B:
                        if k == 1:
                            fold(pb, 0)
                            fold(pb, 1)
                        if k == 5:
                            inverse_root(1, pb)
                        if k == 10:
                            stage_a(pb, 0)
                        if k == 12:
                            stage_a(pb, 1)
                        if k == 19:
                            inverse_root(2, pb)
                        if k == 21:
                            inverse_root(3, pb)
                        if k == 23:
                            hidden_rows(pb, 0)
                            hidden_rows(pb, 1)


_NAMES = ["x", "ctxT", "inproj", "convw", "convb", "xprojT", "dtprojT", "dtb", "alog", "dskip", "wgate", "wup",
          "wdown", "wq", "wk", "bq", "bk", "wfc", "wproj", "eye", "had", "sel"]


def kernel(**inputs):
    import concourse.bacc as bacc
    from concourse.bass_utils import run_bass_kernel_spmd

    a = {k: np.asarray(v) for k, v in inputs.items()}

    def rows(v):
        return v.reshape(B, T, P, -1).transpose(2, 0, 1, 3)

    def halves(v):
        return np.moveaxis(v.reshape((-1, P) + v.shape[1:]), 1, 0)

    def weight(w):
        return halves(w.T).reshape(P, -1)

    xp = a["L0_xattn_x_proj_w"]
    xp = np.concatenate([xp[RANK:], xp[RANK:], xp[RANK:], xp[:RANK]], axis=0)
    h = np.ones((1, 1), np.float32)
    while h.shape[0] < P:
        h = np.block([[h, h], [h, -h]])
    eye = np.eye(P, dtype=np.float32)
    import ml_dtypes
    arrays = {
        "x": rows(a["x"]),
        "ctxT": a["ctx_1024"].transpose(2, 0, 1),
        "inproj": a["L0_xattn_in_proj_w"].T,
        "convw": a["L0_xattn_conv_w"][:, 0, :].T.reshape(1, TAPS, D)[0],
        "convb": halves(a["L0_xattn_conv_b"]),
        "xprojT": halves(xp.T),
        "dtprojT": a["L0_xattn_dt_proj_w"].T,
        "dtb": halves(a["L0_xattn_dt_proj_b"]),
        "alog": halves(a["L0_xattn_A_log"]),
        "dskip": halves(a["L0_xattn_D"]),
        "wgate": weight(a["L0_ffn_w_gate"]),
        "wup": weight(a["L0_ffn_w_up"]),
        "wdown": weight(a["L0_ffn_w_down"]),
        "wq": a["L1_xattn_Wq"].T,
        "wk": a["L1_xattn_Wk"].T,
        "bq": a["L1_xattn_bq"].reshape(P, 1),
        "bk": a["L1_xattn_bk"].reshape(P, 1),
        "wfc": weight(a["L1_ffn_w_fc"]).reshape(P, 2, FF),
        "wproj": weight(a["L1_ffn_w_proj"]).reshape(P, G8, D),
        "eye": eye,
        "had": np.stack([np.concatenate([h, h], 1), np.concatenate([h, -h], 1)], axis=1),
        "sel": np.tile(np.eye(32, dtype=np.float32), (3, 1)).astype(ml_dtypes.bfloat16),
    }
    nc = bacc.Bacc("TRN2", target_bir_lowering=False, num_devices=1)
    feed, args = {}, []
    for name in _NAMES:
        v = np.ascontiguousarray(arrays[name])
        feed[f"in_{name}"] = v
        args.append(nc.dram_tensor(f"in_{name}", v.shape, mybir.dt.from_np(v.dtype), kind="ExternalInput").ap())
    args.append(nc.dram_tensor("out_0", (P, B, T, D), F32, kind="ExternalOutput").ap())
    build(nc, *args)
    r = run_bass_kernel_spmd(nc, [feed], core_ids=[0])
    y = r.results[0]["out_0"]
    return np.ascontiguousarray(y.transpose(1, 2, 0, 3).reshape(B, L, D))
```

```python
from contextlib import ExitStack

import numpy as np

import concourse.bass as bass
from concourse import mybir

F32 = mybir.dt.float32
BF16 = mybir.dt.bfloat16
ALU = mybir.AluOpType
ACT = mybir.ActivationFunctionType
AX = mybir.AxisListType

P = 128
B, L, D = 4, 256, 256
T = L // P
C = 128
NST = 16
TAPS = 4
RANK = 8
FF = 1024
NQ = 4
QUADS = NST // NQ
STEPS = QUADS * T
SPOTS = 12 * STEPS
ROUND = 12582912.0
QB = 128.0
EPS0 = 1e-5
EPS1 = 1e-6
G8 = FF // P


SP = {"conv": -96, "xdbl": -72, "dt": -63, "bb": [-9, 12, 30, 63], "cb": [2, 19, 48, 68], "qk": 174, "energy": 184, "turn_p": 199, "turn_y": 112, "turn_q1": 121, "gate_up": [122, 130, 133, 138], "turn_x": [146, 146, 157, 157], "hadamard": [148, 152, 159, 160], "turn_q2": [168, 168], "down": [180, 181], "turn_x2": 200, "attend": 202, "turn_x3": 218, "fc": [225, 226, 232, 238], "turn_h": [251, 252, 252, 252], "project": [253, 257], "wsum": [68, 74], "act": -74, "xd": -71, "exp": -65, "ln": -56, "zt": -24, "decay": [-5, 1, 7, 13, 24, 35, 52, 63], "aqk": 182, "aexp": 190, "acopy": 199, "copy_q1": 125, "tanh": [125, 132, 135, 138], "copy_x": [145, 146, 158, 158], "quant_y": [156, 156, 164, 164], "copy_q2": [179, 180], "copy_x2": 201, "copy_x3": 222, "gelu": [227, 230, 231, 235], "copy_h": [247, 247, 250, 250], "wabs": [47, 52, 52, 64, 64], "wround": [65, 76, 82, 83, 109], "u": -72, "split": -65, "sp1": -61, "sp2": -51, "zs": -60, "zr": -34, "sz": -17, "amax": 188, "anorm": 191, "gate_y": 110, "x1": 117, "quant1": 121, "gated": [127, 131, 137, 140], "stage_b": [139, 154], "scales2": [154, 163], "quant2": [156, 167], "x2": 179, "x2r": 202, "x3": 211, "scales3": 218, "hstats": [228, 230, 238, 238], "hnorm": [232, 238], "hrange": [243, 246], "hclip": [246, 247], "out": [257, 264], "wscale": [59, 87], "wter": [85, 92, 93, 93, 111], "sum": [20, 34, 44, 57, 64, 74, 80, 106], "fold": [114, 114], "root": [-36, 114, 181, 214], "stage_a": [137, 146], "hrows": [239, 245], "drive": [-1, 7, 20, 24, 44, 57, 76, 77], "scan": [12, 12, 27, 28, 58, 60, 82, 82], "read": [14, 14, 40, 42, 63, 68, 94, 94], "sel": -96, "aneg": -12, "aexpl": -11, "eyeb": -85}


def build(nc, x, ctxT, inproj, convw, convb, xprojT, dtprojT, dtb, alog, dskip, wgate, wup, wdown,
          wq, wk, bq, bk, wfc, wproj, eye, had, sel, out):
    with ExitStack() as ctx:
        def sb(name, shape, dt=F32):
            return ctx.enter_context(nc.sbuf_tensor(name, shape, dt))

        def ps(name):
            return ctx.enter_context(nc.psum_tensor(name, [P, 512], F32))

        def sem(name):
            return ctx.enter_context(nc.semaphore(name))

        X = sb("X", [P, B, T, D])
        CT = sb("CT", [P, B, TAPS - 1 + L])
        INW = sb("INW", [P, D])
        WCONV = sb("WCONV", [P, TAPS, D])
        XPW = sb("XPW", [P, T, 104])
        DTW = sb("DTW", [104, D])
        VEC = sb("VEC", [P, 3, T])
        HALF = sb("HALF", [P, 2, T])
        ALOG = sb("ALOG", [P, T, NST])
        AEXP = sb("AEXP", [P, T, NST])
        ANEG = sb("ANEG", [P, T, NST])
        WQK = sb("WQK", [P, 2, C])
        BQK = sb("BQK", [P, 2])
        EYE = sb("EYE", [P, P])
        EYEB = sb("EYEB", [P, P], BF16)
        HAD = sb("HAD", [P, 2, 2 * P])
        SELC = sb("SELC", [96, 32], BF16)
        SEL = sb("SEL", [96, 32, P], BF16)
        ONES = sb("ONES", [P, P])
        MHALF = sb("MHALF", [P, 4])
        WFC = sb("WFC", [P, 2, FF])
        WPR = sb("WPR", [P, G8, D])
        WG = sb("WG", [P, 2, FF], BF16)
        WU = sb("WU", [P, 2, FF], BF16)
        WD = sb("WD", [P, G8, D], BF16)
        ROUNDC = sb("ROUNDC", [P, 1])
        WSUM = sb("WSUM", [P, 5])
        WMEAN = sb("WMEAN", [P, 5])
        WDIV = sb("WDIV", [P, 5])
        WREC = sb("WREC", [P, 5])
        WSC = sb("WSC", [P, 4])

        CACC = sb("CACC", [P, T, L])
        TH = sb("TH", [P, T, L])
        U2 = sb("U2", [P, 2, T, L])
        XD = sb("XD", [104, L])
        PARTS = sb("PARTS", [96, 2, L], BF16)
        EB, WB = CACC, TH
        LNB = WB
        RES = sb("RES", [P, T, L])
        R1 = RES[0:96, 0, :]
        RELU = sb("RELU", [P, T, L])
        DT = sb("DT", [P, 2, T, L])
        DTU = sb("DTU", [P, 2, T, L])
        ZN = sb("ZN", [P, T, L])
        ZTH = sb("ZTH", [P, T, L])
        SZ = sb("SZ", [P, 2, T, L])
        NDA, NH, NZ = 3, 2, 3
        DA = sb("DA", [P, NDA, NQ, L])
        H = sb("H", [P, NH, NQ, L])
        Z = sb("Z", [P, NZ, NQ, L])
        CW = Z[:, 0, :, :]
        ACC = sb("ACC", [P, T, 2, L])
        PAIR = sb("PAIR", [P, T, 2, L])
        YS = sb("YS", [P, T, L])
        V2 = sb("V2", [P, T, L])

        X1 = sb("X1", [P, T, D])
        X2 = sb("X2", [P, T, D])
        X3 = X2
        XO = sb("XO", [P, T, D])

        STT = sb("STT", [P, 4, T, 6])
        MV = sb("MV", [P, 4, T, 2])
        VE = sb("VE", [P, 4, T])
        RS = sb("RS", [P, 4, T])

        XN = sb("XN", [P, T, D])
        XQ = XN
        XN2 = sb("XN2", [P, T, D])
        D3 = C3 = XN2
        Q1 = sb("Q1", [P, T, D], BF16)
        QT = sb("QT", [P, T, 2, P], BF16)
        AM = sb("AM", [P, T])
        AMC = sb("AMC", [P, T])
        RC = sb("RC", [P, T])
        QS = sb("QS", [P, T])
        GAH = sb("GAH", [P, T])
        KA = sb("KA", [P, T])
        KK = sb("KK", [P, T])
        TG = sb("TG", [P, 2, 512])
        SG = sb("SG", [P, 2, 512])
        XM = sb("XM", [P, T, G8, P])
        HA = sb("HA", [P, T, G8, P])
        HB = XM
        XTS = sb("XTS", [P, T, G8, P])
        AM2 = sb("AM2", [P, T, 2])
        AMX = sb("AMX", [P, T])
        AMT = sb("AMT", [P, T])
        RC2 = sb("RC2", [P, T])
        QS2 = sb("QS2", [P, T])
        DSC = sb("DSC", [P, T])
        YQ = XM[:, :, :, :].rearrange("p t c l -> p t (c l)")
        Q2 = HA[:, 0, :, :].rearrange("p c l -> p (c l)").bitcast(BF16).rearrange("p (t f) -> p t f", t=T)
        Q2T = HA[:, 1, :, :].rearrange("p c l -> p (c l)").bitcast(BF16).rearrange("p (t c l) -> p t c l", t=T, c=G8)

        QK = sb("QK", [P, 2, L])
        NMX = sb("NMX", [P, T])
        EX = sb("EX", [P, T, L])
        RSUM = sb("RSUM", [P, T])
        RINV = sb("RINV", [P, T])
        PN = EX
        AT = sb("AT", [P, T, L])
        X2T = sb("X2T", [P, T, T, P])

        GM = sb("GM", [P, T])
        GI = sb("GI", [P, T])
        GN = sb("GN", [P, T])
        S1 = sb("S1", [P, T])
        X3T = X2T
        HG = sb("HG", [P, T, FF])
        ST3 = sb("ST3", [P, T, 2, 6])
        MV3 = sb("MV3", [P, T, 2])
        VE3 = sb("VE3", [P, T])
        RS3 = sb("RS3", [P, T])
        NM3 = sb("NM3", [P, T])
        MR3 = sb("MR3", [P, T])
        HD = HC = HG
        GM2 = sb("GM2", [P, T])
        NG2 = sb("NG2", [P, T])
        GI2 = sb("GI2", [P, T])
        GN2 = sb("GN2", [P, T])
        S2 = sb("S2", [P, T])
        NG = sb("NG", [P, T])
        HT = sb("HT", [P, T, G8, P])
        WRAW = [w[:, :, :, :].rearrange("p t c l -> p (t c l)") for w in (XM, HA)]
        WRAW.append(HG[:, :, :].rearrange("p t f -> p (t f)"))
        WABS = XTS[:, :, :, :].rearrange("p t c l -> p (t c l)")

        BB = ctx.enter_context(nc.psum_tensor("BB", [P, NQ, L], F32))
        CB = ctx.enter_context(nc.psum_tensor("CB", [P, NQ, L], F32))
        PA = ps("PA")
        R = [ps("R0"), ps("R1"), ps("R2")]

        d_ctx = [sem(f"d_ctx{b}") for b in range(B)]
        d_x = [sem(f"d_x{b}") for b in range(B)]
        d_in, d_cw, d_xp, d_dtw, d_vec, d_alog = (sem(n) for n in (
            "d_in", "d_cw", "d_xp", "d_dtw", "d_vec", "d_alog"))
        d_qk, d_eye, d_had, d_sel = (sem(n) for n in ("d_qk", "d_eye", "d_had", "d_sel"))
        d_w = [sem(f"d_w{i}") for i in range(5)]
        d_out = [sem(f"d_out{b}") for b in range(B)]
        s_const = sem("s_const")
        s_wconv = sem("s_wconv")
        s_aneg = sem("s_aneg")
        s_aexp = sem("s_aexp")
        s_mhalf = sem("s_mhalf")
        s_eyeb = sem("s_eyeb")
        s_sel = sem("s_sel")
        s_wabs = sem("s_wabs")
        s_wtot = sem("s_wtot")
        s_wsc = sem("s_wsc")
        s_wrnd = sem("s_wrnd")
        s_wter = sem("s_wter")

        s_conv = sem("s_conv")
        s_act = sem("s_act")
        s_u = sem("s_u")
        s_xdbl = sem("s_xdbl")
        s_xd = sem("s_xd")
        s_dtp = sem("s_dtp")
        s_parts = sem("s_parts")
        s_ax = sem("s_ax")
        s_e = sem("s_e")
        s_relu = sem("s_relu")
        s_w1e = sem("s_w1e")
        s_ln = sem("s_ln")
        s_res = sem("s_res")
        s_dt = sem("s_dt")
        s_lnst = [sem(f"s_lnst{i}") for i in range(4)]
        s_rstd = [sem(f"s_rstd{i}") for i in range(4)]
        s_zn = sem("s_zn")
        s_zth = sem("s_zth")
        s_sz = sem("s_sz")

        s_bb = sem("s_bb")
        s_cb = sem("s_cb")
        s_da = sem("s_da")
        s_dbu = sem("s_dbu")
        s_scan = sem("s_scan")
        s_z = sem("s_z")
        s_pair = sem("s_pair")
        s_acc = sem("s_acc")
        s_fold = sem("s_fold")

        s_v = sem("s_v")
        s_yT = sem("s_yT")
        s_x1 = sem("s_x1")
        s_xn = sem("s_xn")
        s_am = sem("s_am")
        s_q1 = sem("s_q1")
        s_qT = sem("s_qT")
        s_qTs = sem("s_qTs")
        s_gu = sem("s_gu")
        s_tg = sem("s_tg")
        s_sg = sem("s_sg")
        s_xm = sem("s_xm")
        s_hA = sem("s_hA")
        s_hB = sem("s_hB")
        s_XT = sem("s_XT")
        s_XTs = sem("s_XTs")
        s_Y = sem("s_Y")
        s_am2 = sem("s_am2")
        s_qs2 = sem("s_qs2")
        s_yq = sem("s_yq")
        s_q2 = sem("s_q2")
        s_q2T = sem("s_q2T")
        s_q2Ts = sem("s_q2Ts")
        s_dn = sem("s_dn")
        s_x2 = sem("s_x2")

        s_pqk = sem("s_pqk")
        s_qk = sem("s_qk")
        s_en = sem("s_en")
        s_mx = sem("s_mx")
        s_ex = sem("s_ex")
        s_rinv = sem("s_rinv")
        s_pn = sem("s_pn")
        s_pT = sem("s_pT")
        s_AT = sem("s_AT")
        s_xn2 = sem("s_xn2")
        s_x2T = sem("s_x2T")
        s_x2Ts = sem("s_x2Ts")
        s_pxm = sem("s_pxm")
        s_x3 = sem("s_x3")

        s_d3 = sem("s_d3")
        s_gm = sem("s_gm")
        s_c3 = sem("s_c3")
        s_x3T = sem("s_x3T")
        s_x3Ts = sem("s_x3Ts")
        s_fc = sem("s_fc")
        s_h = sem("s_h")
        s_st3 = sem("s_st3")
        s_mv3 = sem("s_mv3")
        s_rs3 = sem("s_rs3")
        s_mr3 = sem("s_mr3")
        s_hd = sem("s_hd")
        s_gm2 = sem("s_gm2")
        s_hc = sem("s_hc")
        s_hT = sem("s_hT")
        s_hTs = sem("s_hTs")
        s_pj = sem("s_pj")
        s_o = sem("s_o")

        block = ctx.enter_context(nc.Block())

        @block.sync
        def _(sync):
            for b in range(B):
                sync.dma_start(CT[:, b, TAPS - 1:], ctxT[:, b, :]).then_inc(d_ctx[b], 16)
                if b == 0:
                    sync.dma_start(INW[:, :], inproj).then_inc(d_in, 16)
                    sync.dma_start(CW, convw.partition_broadcast(P)).then_inc(d_cw, 16)
                    sync.dma_start(VEC[:, 0, :], convb).then_inc(d_vec, 16)
                    sync.dma_start(VEC[:, 1, :], dtb).then_inc(d_vec, 16)
                    sync.dma_start(VEC[:, 2, :], dskip).then_inc(d_vec, 16)
                    sync.dma_start(XPW[:, :, :], xprojT).then_inc(d_xp, 16)
                    sync.dma_start(DTW[96:104, :], dtprojT).then_inc(d_dtw, 16)
                    sync.dma_start(ALOG[:, :, :], alog).then_inc(d_alog, 16)
                    sync.dma_start(SELC[:, :], sel).then_inc(d_sel, 16)
                sync.dma_start(X[:, b, :, :], x[:, b, :, :]).then_inc(d_x[b], 16)
            sync.dma_start(EYE[:, :], eye).then_inc(d_eye, 16)
            sync.dma_start(WQK[:, 0, :], wq).then_inc(d_qk, 16)
            sync.dma_start(WQK[:, 1, :], wk).then_inc(d_qk, 16)
            sync.dma_start(BQK[:, 0:1], bq).then_inc(d_qk, 16)
            sync.dma_start(BQK[:, 1:2], bk).then_inc(d_qk, 16)
            sync.dma_start(WRAW[0], wgate).then_inc(d_w[0], 16)
            sync.dma_start(WRAW[1], wup).then_inc(d_w[1], 16)
            sync.dma_start(WRAW[2], wdown).then_inc(d_w[2], 16)
            sync.dma_start(HAD[:, :, :], had).then_inc(d_had, 16)
            sync.dma_start(WFC[:, :, :], wfc).then_inc(d_w[3], 16)
            sync.dma_start(WPR[:, :, :], wproj).then_inc(d_w[4], 16)
            for b in range(B):
                for t in range(T):
                    sync.wait_ge(s_o, T * b + t + 1)
                    sync.dma_start(out[:, b, t, :], XO[:, t, :]).then_inc(d_out[b], 16)
            for b in range(B):
                sync.wait_ge(d_out[b], 16 * T)

        @block.tensor
        def _(pe):
            def prep_conv(b):
                pe.wait_ge(d_ctx[b], 16)
                pe.wait_ge(s_wconv, 1)
                pe.wait_ge(s_const, 4)
                if b > 0:
                    pe.wait_ge(s_relu, 2 * b)
                    pe.wait_ge(s_ax, 2 * b)
                for c in range(T):
                    for k in range(TAPS):
                        mm = pe.matmul(PA[:, c * L:(c + 1) * L], WCONV[:, k, c * P:(c + 1) * P],
                                       CT[:, b, k:k + L], start=(k == 0), stop=(k == TAPS - 1))
                mm.then_inc(s_conv, 1)

            def prep_xdbl(b):
                pe.wait_ge(s_u, b + 1)
                pe.wait_ge(d_xp, 16)
                for c in range(T):
                    mm = pe.matmul(PA[0:104, 0:L], XPW[:, c, :], U2[:, b % 2, c, :],
                                   start=(c == 0), stop=(c == T - 1))
                mm.then_inc(s_xdbl, 1)

            def prep_dt(b):
                pe.wait_ge(s_xd, b + 1)
                pe.wait_ge(d_dtw, 16)
                for c in range(T):
                    mm = pe.matmul(PA[:, c * L:(c + 1) * L], DTW[96:104, c * P:(c + 1) * P],
                                   XD[96:104, :], start=True, stop=True)
                mm.then_inc(s_dtp, 1)

            def bcast_b(b, q):
                if q == 0:
                    pe.wait_ge(s_parts, 4 * (b + 1))
                    pe.wait_ge(s_sel, 1)
                g = STEPS * b + T * q
                if g:
                    pe.wait_ge(s_dbu, g)
                for n in range(NQ):
                    mm = pe.matmul(BB[:, n, :], SEL[:, NQ * q + n, :],
                                   PARTS[:, b % 2, :], start=True, stop=True)
                mm.then_inc(s_bb, 1)

            def bcast_c(b, q):
                g = STEPS * b + T * q
                if g:
                    pe.wait_ge(s_z, g)
                for n in range(NQ):
                    mm = pe.matmul(CB[:, n, :], SEL[:, NST + NQ * q + n, :],
                                   PARTS[:, b % 2, :], start=True, stop=True)
                mm.then_inc(s_cb, 1)

            def attn_qk(b):
                pe.wait_ge(d_qk, 64)
                if b > 0:
                    pe.wait_ge(s_o, T * b)
                else:
                    pe.wait_ge(s_wsc, 10)
                for i in range(2):
                    mm = pe.matmul(R[2][:, i * L:(i + 1) * L], WQK[:, i, :], CT[:, b, TAPS - 1:],
                                   start=True, stop=True)
                mm.then_inc(s_pqk, 1)

            def attn_energy(b):
                pe.wait_ge(s_qk, 2 * (b + 1))
                for t in range(T):
                    mm = pe.matmul(R[2][:, t * L:(t + 1) * L], QK[:, 0, t * P:(t + 1) * P], QK[:, 1, :],
                                   start=True, stop=True)
                mm.then_inc(s_en, 1)

            def attn_turn(b):
                pe.wait_ge(s_pn, 2 * (b + 1))
                pe.wait_ge(d_eye, 16)
                for c in range(T):
                    for t in range(T):
                        mm = pe.transpose(R[2][:, c * L + t * P:c * L + (t + 1) * P],
                                          PN[:, t, c * P:(c + 1) * P], EYE[:, :])
                mm.then_inc(s_pT, 1)

            def weight_sums(first, n):
                pe.wait_ge(s_wabs, first + n)
                pe.wait_ge(s_const, 4)
                if first:
                    pe.wait_ge(s_wsc, 5)
                pe.matmul(R[2][:, 0:n], ONES[:, :], WSUM[:, first:first + n],
                          start=True, stop=True).then_inc(s_wtot, 1)

            def turn_y(b):
                pe.wait_ge(s_v, 3 * (b + 1))
                if b > 0:
                    pe.wait_ge(s_x2, 2 * b - 1)
                for t in range(T):
                    for c in range(T):
                        mm = pe.transpose(R[0][:, t * D + c * P:t * D + (c + 1) * P],
                                          V2[:, c, t * P:(t + 1) * P], EYE[:, :])
                mm.then_inc(s_yT, 1)

            def turn_q1(b):
                pe.wait_ge(s_q1, 3 * (b + 1))
                pe.wait_ge(s_eyeb, 1)
                if b > 0:
                    pe.wait_ge(s_x2, 2 * b)
                r = R[1][:, 0:256].bitcast(BF16)
                for t in range(T):
                    for k in range(2):
                        j = (t * 2 + k) * P
                        mm = pe.transpose(r[:, j:j + P], Q1[:, t, k * P:(k + 1) * P], EYEB[:, :])
                mm.then_inc(s_qT, 1)

            def gate_up(b, j):
                t, i = j // 2, j % 2
                if j == 0:
                    pe.wait_ge(s_qTs, b + 1)
                    if b == 0:
                        pe.wait_ge(s_wter, 4)
                    pe.wait_ge(s_x1, b + 1)
                else:
                    pe.wait_ge(s_xm, 4 * b + j)
                for w, r in ((WG, R[0]), (WU, R[1])):
                    for k in range(2):
                        mm = pe.matmul(r[:, :], QT[:, t, k, :], w[:, k, i * 512:(i + 1) * 512],
                                       start=(k == 0), stop=(k == 1))
                mm.then_inc(s_gu, 1)

            def turn_x(b, j):
                t, i = j // 2, j % 2
                pe.wait_ge(s_hB, 4 * b + 2 * t + 2)
                if t == 0:
                    pe.wait_ge(s_xm, 4 * (b + 1))
                else:
                    pe.wait_ge(s_yq, 4 * b + i + 1)
                for c in range(4):
                    mm = pe.transpose(R[i][:, c * P:(c + 1) * P], HB[:, t, 4 * i + c, :], EYE[:, :])
                mm.then_inc(s_XT, 1)

            def hadamard(b, j):
                t, i = j // 2, j % 2
                pe.wait_ge(s_XTs, 4 * b + j + 1)
                pe.wait_ge(d_had, 16)
                for p in range(2):
                    for e in range(2):
                        mm = pe.matmul(R[i][:, p * 2 * P:(p + 1) * 2 * P], XTS[:, t, 4 * i + 2 * p + e, :],
                                       HAD[:, e, :], start=(e == 0), stop=(e == 1))
                mm.then_inc(s_Y, 1)

            def turn_q2(b, t):
                pe.wait_ge(s_q2, 2 * b + t + 1)
                pe.wait_ge(s_yq, 4 * b + 3 + t)
                r = R[t][:, :].bitcast(BF16)
                for c in range(G8):
                    mm = pe.transpose(r[:, c * P:(c + 1) * P], Q2[:, t, c * P:(c + 1) * P], EYEB[:, :])
                mm.then_inc(s_q2T, 1)

            def down(b, t):
                pe.wait_ge(s_q2Ts, 2 * b + t + 1)
                if b == 0:
                    pe.wait_ge(s_wter, 6)
                for c in range(G8):
                    mm = pe.matmul(R[t][:, 0:D], Q2T[:, t, c, :], WD[:, c, :],
                                   start=(c == 0), stop=(c == G8 - 1))
                mm.then_inc(s_dn, 1)

            def turn_x2(b):
                pe.wait_ge(s_xn2, 2 * (b + 1))
                pe.wait_ge(s_AT, b + 1)
                for c in range(T):
                    for t in range(T):
                        j = (c * T + t) * P
                        mm = pe.transpose(R[2][:, j:j + P], XN2[:, t, c * P:(c + 1) * P], EYE[:, :])
                mm.then_inc(s_x2T, 1)

            def attend(b):
                pe.wait_ge(s_x2Ts, b + 1)
                for t in range(T):
                    for c in range(T):
                        mm = pe.matmul(R[2][:, t * D:(t + 1) * D], X2T[:, c, t, :], AT[:, c, :],
                                       start=(c == 0), stop=(c == T - 1))
                mm.then_inc(s_pxm, 1)

            def turn_x3(b):
                pe.wait_ge(s_c3, b + 1)
                for c in range(T):
                    for t in range(T):
                        j = (c * T + t) * P
                        mm = pe.transpose(R[2][:, j:j + P], C3[:, t, c * P:(c + 1) * P], EYE[:, :])
                mm.then_inc(s_x3T, 1)

            def fc(b, j):
                t, i = j // 2, j % 2
                if j == 0:
                    pe.wait_ge(s_x3Ts, b + 1)
                    if b == 0:
                        pe.wait_ge(s_wter, 10)
                else:
                    pe.wait_ge(s_h, 4 * b + j)
                for k in range(2):
                    mm = pe.matmul(R[2][:, :], X3T[:, k, t, :], WFC[:, k, i * 512:(i + 1) * 512],
                                   start=(k == 0), stop=(k == 1))
                mm.then_inc(s_fc, 1)

            def turn_h(b, j):
                t, i = j // 2, j % 2
                pe.wait_ge(s_hc, 2 * b + t + 1)
                if j == 0:
                    pe.wait_ge(s_h, 4 * b + 4)
                else:
                    pe.wait_ge(s_hTs, 4 * b + j)
                for c in range(4):
                    mm = pe.transpose(R[2][:, c * P:(c + 1) * P],
                                      HC[:, t, (4 * i + c) * P:(4 * i + c + 1) * P], EYE[:, :])
                mm.then_inc(s_hT, 1)

            def project(b, t):
                if t == 0:
                    pe.wait_ge(s_hTs, 4 * b + 4)
                else:
                    pe.wait_ge(s_o, 2 * b + 1)
                for c in range(G8):
                    mm = pe.matmul(R[2][:, 0:D], HT[:, t, c, :], WPR[:, c, :],
                                   start=(c == 0), stop=(c == G8 - 1))
                mm.then_inc(s_pj, 1)

            plan = [(bcast_b, SP["bb"][q], q) for q in range(QUADS)]
            plan += [(bcast_c, SP["cb"][q], q) for q in range(QUADS)]
            plan += [(prep_conv, SP["conv"]), (prep_xdbl, SP["xdbl"]), (prep_dt, SP["dt"]),
                     (attn_qk, SP["qk"]), (attn_energy, SP["energy"]), (attn_turn, SP["turn_p"])]
            plan += [(turn_h, SP["turn_h"][j], j) for j in range(4)]
            plan += [(project, SP["project"][t], t) for t in range(T)]
            plan += [(turn_y, SP["turn_y"]), (turn_q1, SP["turn_q1"])]
            plan += [(gate_up, SP["gate_up"][j], j) for j in range(4)]
            plan += [(turn_x, SP["turn_x"][j], j) for j in range(4)]
            plan += [(hadamard, SP["hadamard"][j], j) for j in range(4)]
            for t in range(T):
                plan += [(turn_q2, SP["turn_q2"][t], t), (down, SP["down"][t], t)]
            plan += [(turn_x2, SP["turn_x2"]), (attend, SP["attend"]), (turn_x3, SP["turn_x3"])]
            plan += [(fc, SP["fc"][j], j) for j in range(4)]
            for u in range(-SPOTS, SPOTS * (B + 4)):
                if u == SP["wsum"][0]:
                    weight_sums(0, 3)
                if u == SP["wsum"][1]:
                    weight_sums(3, 2)
                for fn, spot, *args in plan:
                    b, r = divmod(u - spot, SPOTS)
                    if r == 0 and 0 <= b < B:
                        fn(b, *args)

        @block.scalar
        def _(act):
            def prep_act(b):
                act.wait_ge(s_conv, b + 1)
                act.wait_ge(d_vec, 48)
                act.wait_ge(s_wconv, 3)
                if b > 0:
                    act.wait_ge(s_w1e, 2 * b)
                    act.wait_ge(s_dt, 2 * b)
                for c in range(T):
                    act.activation(CACC[:, c, :], PA[:, c * L:(c + 1) * L], ACT.Identity,
                                   bias=VEC[:, 0, c:c + 1]).then_inc(s_act, 1)
                    act.activation(TH[:, c, :], PA[:, c * L:(c + 1) * L], ACT.Tanh,
                                   bias=HALF[:, 0, c:c + 1], scale=0.5).then_inc(s_act, 1)

            def prep_xd(b):
                act.wait_ge(s_xdbl, b + 1)
                if b > 0:
                    act.wait_ge(s_dtp, b)
                    act.wait_ge(s_parts, 4 * b)
                act.activation(XD[:, :], PA[0:104, 0:L], ACT.Copy, scale=0.5).then_inc(s_xd, 1)

            def prep_exp(b):
                act.wait_ge(s_dtp, b + 1)
                if b > 0:
                    act.wait_ge(s_w1e, 2 * b)
                for c in range(T):
                    act.activation(EB[:, c, :], PA[:, c * L:(c + 1) * L], ACT.Abs,
                                   bias=VEC[:, 1, c:c + 1]).then_inc(s_ax, 1)
                act.wait_ge(s_ax, 2 * (b + 1))
                act.activation(EB[:, :, :], EB[:, :, :], ACT.Exp, scale=-1.0).then_inc(s_e, 1)

            def prep_ln(b):
                act.wait_ge(s_w1e, 2 * b + 2)
                act.activation(LNB[:, :, :], WB[:, :, :], ACT.Ln).then_inc(s_ln, 1)

            def prep_z(b):
                act.wait_ge(s_zn, 2 * (b + 1))
                if b > 0:
                    act.wait_ge(s_sz, b)
                act.activation(ZTH[:, :, :], ZN[:, :, :], ACT.Tanh, scale=0.5).then_inc(s_zth, 1)

            def decay(b, s):
                g = STEPS * b + s
                q, c = s // T, s % T
                if s == 0:
                    act.wait_ge(s_dt, 2 * b + 1)
                    if b == 0:
                        act.wait_ge(s_aneg, 1)
                        act.wait_ge(s_const, 4)
                if g >= NDA:
                    act.wait_ge(s_scan, g - NDA + 1)
                for n in range(NQ):
                    i = act.activation(DA[:, g % NDA, n, 1:L], DT[:, b % 2, c, 1:L], ACT.Exp,
                                       scale=ANEG[:, c, NQ * q + n:NQ * q + n + 1])
                i.then_inc(s_da, 1)

            def attn_qk(b):
                act.wait_ge(s_pqk, b + 1)
                if b > 0:
                    act.wait_ge(s_en, b)
                for i in range(2):
                    act.activation(QK[:, i, :], R[2][:, i * L:(i + 1) * L], ACT.Identity,
                                   bias=BQK[:, i:i + 1]).then_inc(s_qk, 1)

            def attn_exp(b):
                act.wait_ge(s_mx, b + 1)
                if b > 0:
                    act.wait_ge(s_pn, 2 * b)
                for t in range(T):
                    act.activation(EX[:, t, :], R[2][:, t * L:(t + 1) * L], ACT.Exp, bias=NMX[:, t:t + 1],
                                   accum_out=RSUM[:, t:t + 1]).then_inc(s_ex, 1)

            def attn_copy(b):
                act.wait_ge(s_pT, b + 1)
                if b > 0:
                    act.wait_ge(s_pxm, b)
                act.activation(AT[:, :, :], R[2][:, :].rearrange("p (c l) -> p c l", c=T),
                               ACT.Copy).then_inc(s_AT, 1)

            def weight_src(i):
                return (WRAW[0], WRAW[1], WRAW[2],
                        WFC[:, :, :].rearrange("p k f -> p (k f)"),
                        WPR[:, :, :].rearrange("p k f -> p (k f)"))[i]

            def weight_abs(i):
                act.wait_ge(d_w[i], 16)
                if i:
                    act.wait_ge(s_wabs, i)
                act.activation(WABS, weight_src(i), ACT.Abs,
                               accum_out=WSUM[:, i:i + 1]).then_inc(s_wabs, 1)

            def weight_round(i):
                act.wait_ge(s_const, 4)
                act.wait_ge(s_wsc, 5 if i < 3 else 10)
                act.activation(weight_src(i), weight_src(i), ACT.Identity, bias=ROUNDC[:, 0:1],
                               scale=WREC[:, i:i + 1]).then_inc(s_wrnd, 1)

            def copy_q1(b):
                act.wait_ge(s_qT, b + 1)
                if b > 0:
                    act.wait_ge(s_gu, 4 * b)
                act.activation(QT[:, :, :, :].rearrange("p a b c -> p (a b c)"),
                               R[1][:, 0:256].bitcast(BF16), ACT.Copy).then_inc(s_qTs, 1)

            def gate_tanh(b, j):
                act.wait_ge(s_gu, 4 * b + j + 1)
                act.wait_ge(s_am, 7 * (b + 1))
                if 4 * b + j >= 2:
                    act.wait_ge(s_sg, 4 * b + j - 1)
                act.activation(TG[:, j % 2, :], R[0][:, :], ACT.Tanh,
                               scale=GAH[:, j // 2:j // 2 + 1]).then_inc(s_tg, 1)

            def copy_x(b, j):
                t, i = j // 2, j % 2
                act.wait_ge(s_XT, 4 * b + j + 1)
                if b > 0:
                    act.wait_ge(s_Y, 4 * b)
                act.activation(XTS[:, t, 4 * i:4 * i + 4, :], R[i][:, :].rearrange(
                    "p (c l) -> p c l", c=4), ACT.Copy).then_inc(s_XTs, 1)

            def quant_y(b, j):
                t, i = j // 2, j % 2
                act.wait_ge(s_qs2, 10 * b + 5 * t + 5)
                act.activation(YQ[:, t, i * 512:(i + 1) * 512], R[i][:, :], ACT.Identity,
                               bias=ROUNDC[:, 0:1], scale=QS2[:, t:t + 1]).then_inc(s_yq, 1)

            def copy_q2(b, t):
                act.wait_ge(s_q2T, 2 * b + t + 1)
                act.wait_ge(s_hB, 4 * (b + 1))
                if b > 0:
                    act.wait_ge(s_dn, 2 * b)
                act.activation(Q2T[:, t, :, :].rearrange("p c l -> p (c l)"), R[t][:, :].bitcast(BF16),
                               ACT.Copy).then_inc(s_q2Ts, 1)

            def copy_x2(b):
                act.wait_ge(s_x2T, b + 1)
                if b > 0:
                    act.wait_ge(s_fc, 4 * b)
                act.activation(X2T[:, :, :, :].rearrange("p a b c -> p (a b c)"), R[2][:, :],
                               ACT.Copy).then_inc(s_x2Ts, 1)

            def copy_x3(b):
                act.wait_ge(s_x3T, b + 1)
                act.wait_ge(s_pxm, b + 1)
                act.activation(X3T[:, :, :, :].rearrange("p a b c -> p (a b c)"), R[2][:, :],
                               ACT.Copy).then_inc(s_x3Ts, 1)

            def gelu(b, j):
                t, i = j // 2, j % 2
                act.wait_ge(s_fc, 4 * b + j + 1)
                if b > 0:
                    act.wait_ge(s_hT, 4 * b)
                act.activation(HG[:, t, i * 512:(i + 1) * 512], R[2][:, :], ACT.Gelu,
                               scale=S1[:, t:t + 1]).then_inc(s_h, 1)

            def copy_h(b, j):
                t, i = j // 2, j % 2
                act.wait_ge(s_hT, 4 * b + j + 1)
                if b > 0:
                    act.wait_ge(s_pj, 2 * b)
                act.activation(HT[:, t, 4 * i:4 * i + 4, :], R[2][:, :].rearrange(
                    "p (c l) -> p c l", c=4), ACT.Copy).then_inc(s_hTs, 1)

            act.wait_ge(d_alog, 16)
            plan = [(prep_act, SP["act"]), (prep_xd, SP["xd"]), (prep_exp, SP["exp"])]
            plan += [(decay, SP["decay"][n], n) for n in range(STEPS)]
            plan += [(prep_ln, SP["ln"]), (prep_z, SP["zt"]),
                     (attn_qk, SP["aqk"]), (attn_exp, SP["aexp"]), (attn_copy, SP["acopy"])]
            plan += [(copy_h, SP["copy_h"][j], j) for j in range(4)]
            plan += [(copy_q1, SP["copy_q1"])]
            plan += [(gate_tanh, SP["tanh"][j], j) for j in range(4)]
            plan += [(copy_x, SP["copy_x"][j], j) for j in range(4)]
            plan += [(quant_y, SP["quant_y"][j], j) for j in range(4)]
            plan += [(copy_q2, SP["copy_q2"][t], t) for t in range(T)]
            plan += [(copy_x2, SP["copy_x2"]), (copy_x3, SP["copy_x3"])]
            plan += [(gelu, SP["gelu"][j], j) for j in range(4)]
            for u in range(-SPOTS, SPOTS * (B + 4)):
                if u == SP["aexpl"]:
                    act.wait_ge(d_alog, 16)
                    act.activation(AEXP[:, :, :], ALOG[:, :, :], ACT.Exp).then_inc(s_aexp, 1)
                for i in range(5):
                    if u == SP["wabs"][i]:
                        weight_abs(i)
                    if u == SP["wround"][i]:
                        weight_round(i)
                for fn, spot, *args in plan:
                    b, r = divmod(u - spot, SPOTS)
                    if r == 0 and 0 <= b < B:
                        fn(b, *args)

        @block.vector
        def _(dve):
            def norm_stats(i, b, src, scale, add):
                for t in range(T):
                    dve.bn_stats(STT[:, i, t, :], src[:, t, :]).then_inc(s_lnst[i], 1)
                for t in range(T):
                    dve.wait_ge(s_lnst[i], 5 * b + t + 1)
                    dve.bn_aggr(MV[:, i, t, :], STT[:, i, t, :]).then_inc(s_lnst[i], 1)
                dve.wait_ge(s_lnst[i], 5 * b + 4)
                dve.tensor_scalar(VE[:, i, :], MV[:, i, :, 1], scale, add, ALU.mult, ALU.add)\
                    .then_inc(s_lnst[i], 1)

            def norm_rows(i, b, src, dst, done):
                dve.wait_ge(s_rstd[i], b + 1)
                for t in range(T):
                    dve.tensor_scalar(dst[:, t, :], src[:, t, :], MV[:, i, t, 0:1], RS[:, i, t:t + 1],
                                      ALU.subtract, ALU.mult).then_inc(done, 1)

            def prep_u(b):
                dve.wait_ge(s_act, 4 * (b + 1))
                if b > 1:
                    dve.wait_ge(s_v, 3 * (b - 1))
                dve.scalar_tensor_tensor(out=U2[:, b % 2, :, :], in0=TH[:, :, :], scalar=1.0,
                                         in1=CACC[:, :, :], op0=ALU.add, op1=ALU.mult).then_inc(s_u, 1)

            def prep_split(b):
                pt = PARTS[:, b % 2, :]
                dve.wait_ge(s_xd, b + 1)
                if b > 1:
                    dve.wait_ge(s_cb, QUADS * (b - 1))
                dve.tensor_copy(pt, XD[0:96, :]).then_inc(s_parts, 1)
                dve.wait_ge(s_parts, 4 * b + 1)
                dve.tensor_tensor(R1, XD[0:96, :], pt, ALU.subtract).then_inc(s_parts, 1)
                dve.wait_ge(s_parts, 4 * b + 2)
                dve.tensor_copy(pt[32:64, :], R1[32:64, :])
                dve.tensor_copy(pt[64:96, :], R1[64:96, :]).then_inc(s_parts, 1)
                dve.wait_ge(s_parts, 4 * b + 3)
                dve.tensor_tensor(pt[64:96, :], R1[64:96, :], pt[64:96, :], ALU.subtract).then_inc(s_parts, 1)

            def prep_softplus1(b):
                dve.wait_ge(s_ax, 2 * (b + 1))
                for c in range(T):
                    dve.tensor_scalar(RELU[:, c, :], PA[:, c * L:(c + 1) * L], VEC[:, 1, c:c + 1], 0.0,
                                      ALU.add, ALU.max).then_inc(s_relu, 1)
                dve.wait_ge(s_e, b + 1)
                dve.tensor_scalar(WB[:, :, :], EB[:, :, :], 1.0, None, ALU.add).then_inc(s_w1e, 1)
                dve.wait_ge(s_w1e, 2 * b + 1)
                dve.scalar_tensor_tensor(out=RES[:, :, :], in0=WB[:, :, :], scalar=-1.0, in1=EB[:, :, :],
                                         op0=ALU.add, op1=ALU.subtract).then_inc(s_w1e, 1)
                dve.wait_ge(s_w1e, 2 * b + 2)
                dve.wait_ge(s_relu, 2 * b + 2)
                dve.tensor_tensor(RELU[:, :, :], RELU[:, :, :], RES[:, :, :], ALU.subtract).then_inc(s_res, 1)

            def prep_softplus2(b):
                dve.wait_ge(s_ln, b + 1)
                dve.wait_ge(s_res, b + 1)
                if b > 1:
                    dve.wait_ge(s_da, STEPS * (b - 1))
                dve.tensor_tensor(DT[:, b % 2, :, :], LNB[:, :, :], RELU[:, :, :], ALU.add).then_inc(s_dt, 1)
                dve.wait_ge(s_dt, 2 * b + 1)
                dve.scalar_tensor_tensor(out=DTU[:, b % 2, :, :], in0=DT[:, b % 2, :, :], scalar=0.5,
                                         in1=U2[:, b % 2, :, :], op0=ALU.mult, op1=ALU.mult).then_inc(s_dt, 1)

            def prep_sz(b):
                dve.wait_ge(s_zth, b + 1)
                dve.scalar_tensor_tensor(out=SZ[:, b % 2, :, :], in0=ZTH[:, :, :], scalar=1.0,
                                         in1=ZN[:, :, :], op0=ALU.add, op1=ALU.mult).then_inc(s_sz, 1)

            def drive(b, s):
                g, q, c = STEPS * b + s, s // T, s % T
                dve.wait_ge(s_dt, 2 * (b + 1))
                dve.wait_ge(s_bb, QUADS * b + q + 1)
                if g >= NH:
                    dve.wait_ge(s_z, g - NH + 1)
                dve.tensor_tensor(H[:, g % NH, :, :], BB[:, :, :],
                                  DTU[:, b % 2, c, :].unsqueeze(1).to_broadcast([P, NQ, L]),
                                  ALU.mult).then_inc(s_dbu, 1)

            def scan(b, s):
                g = STEPS * b + s
                dve.wait_ge(s_da, g + 1)
                dve.wait_ge(s_dbu, g + 1)
                hh = H[:, g % NH, :, :].rearrange("p n l -> p (n l)")
                dve.tensor_tensor_scan(hh, DA[:, g % NDA, :, :].rearrange("p n l -> p (n l)"), hh, 0.0,
                                       ALU.mult, ALU.add).then_inc(s_scan, 1)

            def read_out(b, s):
                g, q = STEPS * b + s, s // T
                dve.wait_ge(s_scan, g + 1)
                dve.wait_ge(s_cb, QUADS * b + q + 1)
                if g >= NZ:
                    dve.wait_ge(s_pair, g - NZ + 1)
                dve.tensor_tensor(Z[:, g % NZ, :, :], CB[:, :, :], H[:, g % NH, :, :], ALU.mult)\
                    .then_inc(s_z, 1)

            def attn_max(b):
                dve.wait_ge(s_en, b + 1)
                if b > 0:
                    dve.wait_ge(s_ex, 2 * b)
                dve.tensor_reduce(NMX[:, :], R[2][:, :].rearrange("p (t l) -> p t l", t=T), AX.X, ALU.max,
                                  negate=True).then_inc(s_mx, 1)

            def attn_norm(b):
                dve.wait_ge(s_ex, 2 * (b + 1))
                dve.reciprocal(RINV[:, :], RSUM[:, :]).then_inc(s_rinv, 1)
                dve.wait_ge(s_rinv, b + 1)
                if b > 0:
                    dve.wait_ge(s_pT, b)
                for t in range(T):
                    dve.tensor_scalar(PN[:, t, :], EX[:, t, :], RINV[:, t:t + 1], None, ALU.mult)\
                        .then_inc(s_pn, 1)

            def weight_scales(first, n):
                dve.wait_ge(s_wtot, 1 if first == 0 else 2)
                cols = slice(first, first + n)
                w = 5 if first else 0
                if first == 0:
                    dve.tensor_scalar(WMEAN[:, cols], R[2][:, 0:n], 1.0 / (FF * D), EPS0, ALU.mult, ALU.max)\
                        .then_inc(s_wsc, 1)
                    dve.wait_ge(s_wsc, 1)
                    dve.reciprocal(WREC[:, cols], WMEAN[:, cols]).then_inc(s_wsc, 1)
                    dve.tensor_scalar(WSC[:, 0:1], WMEAN[:, 0:1], 1.0 / (2 * QB), None, ALU.mult)\
                        .then_inc(s_wsc, 1)
                    dve.scalar_tensor_tensor(out=WSC[:, 1:2], in0=WMEAN[:, 0:1], scalar=1.0 / (64 * QB * QB),
                                             in1=WMEAN[:, 1:2], op0=ALU.mult, op1=ALU.mult).then_inc(s_wsc, 1)
                    dve.tensor_scalar(WSC[:, 2:3], WMEAN[:, 2:3], 1.0 / QB, None, ALU.mult).then_inc(s_wsc, 1)
                else:
                    dve.tensor_scalar(WMEAN[:, cols], R[2][:, 0:n], 1.0 / (FF * D), None, ALU.mult)\
                        .then_inc(s_wsc, 1)
                    dve.wait_ge(s_wsc, w + 1)
                    dve.tensor_scalar(WDIV[:, cols], WMEAN[:, cols], EPS1, None, ALU.add).then_inc(s_wsc, 1)
                    dve.wait_ge(s_wsc, w + 2)
                    dve.reciprocal(WREC[:, cols], WDIV[:, cols]).then_inc(s_wsc, 3)

            def weight_ternary(i):
                src = (WRAW[0], WRAW[1], WRAW[2],
                       WFC[:, :, :].rearrange("p k f -> p (k f)"), WPR[:, :, :].rearrange("p k f -> p (k f)"))[i]
                dst = (WG, WU, WD, WFC, WPR)[i][:, :, :].rearrange("p k f -> p (k f)")
                dve.wait_ge(s_wrnd, i + 1)
                dve.tensor_scalar(dst, src, ROUND, 1.0, ALU.subtract, ALU.min).then_inc(s_wter, 1)
                dve.wait_ge(s_wter, 2 * i + 1)
                dve.tensor_scalar(dst, dst, -1.0, None, ALU.max).then_inc(s_wter, 1)

            def gate_y(b):
                dve.wait_ge(s_fold, 2 * (b + 1))
                if b > 0:
                    dve.wait_ge(s_yT, b)
                for c in range(T):
                    dve.scalar_tensor_tensor(out=YS[:, c, :], in0=U2[:, b % 2, c, :], scalar=HALF[:, 1, c:c + 1],
                                             in1=YS[:, c, :], op0=ALU.mult, op1=ALU.add).then_inc(s_v, 1)
                dve.wait_ge(s_v, 3 * b + 2)
                dve.wait_ge(s_sz, b + 1)
                dve.tensor_tensor(V2[:, :, :], YS[:, :, :], SZ[:, b % 2, :, :], ALU.mult).then_inc(s_v, 1)

            def rows_x1(b):
                dve.wait_ge(s_yT, b + 1)
                dve.scalar_tensor_tensor(out=X1[:, :, :], in0=R[0][:, :].rearrange("p (t d) -> p t d", t=T),
                                         scalar=0.5, in1=X[:, b, :, :], op0=ALU.mult, op1=ALU.add)\
                    .then_inc(s_x1, 1)
                dve.wait_ge(s_x1, b + 1)
                norm_stats(1, b, X1, 1.0, EPS0)

            def quant1(b):
                norm_rows(1, b, X1, XN, s_xn)
                dve.wait_ge(s_xn, 2 * (b + 1))
                a = 7 * b
                if b > 0:
                    dve.wait_ge(s_tg, 4 * b)
                dve.tensor_reduce(AM[:, :], XN[:, :, :], AX.X, ALU.max, apply_absolute_value=True)\
                    .then_inc(s_am, 1)
                dve.wait_ge(s_am, a + 1)
                dve.tensor_scalar(AMC[:, :], AM[:, :], EPS0, None, ALU.max).then_inc(s_am, 1)
                dve.wait_ge(s_am, a + 2)
                dve.reciprocal(RC[:, :], AMC[:, :]).then_inc(s_am, 1)
                dve.tensor_scalar(GAH[:, :], AMC[:, :], WSC[:, 0:1], None, ALU.mult).then_inc(s_am, 1)
                dve.tensor_scalar(KA[:, :], AMC[:, :], WSC[:, 1:2], None, ALU.mult).then_inc(s_am, 1)
                dve.wait_ge(s_am, a + 5)
                dve.tensor_scalar(QS[:, :], RC[:, :], QB, None, ALU.mult).then_inc(s_am, 1)
                dve.tensor_tensor(KK[:, :], KA[:, :], AMC[:, :], ALU.mult).then_inc(s_am, 1)
                dve.wait_ge(s_am, a + 6)
                for t in range(T):
                    dve.tensor_scalar(XQ[:, t, :], XN[:, t, :], QS[:, t:t + 1], QB - 1, ALU.mult, ALU.min)\
                        .then_inc(s_q1, 1)
                dve.wait_ge(s_q1, 3 * b + 2)
                if b > 0:
                    dve.wait_ge(s_qT, b)
                dve.tensor_scalar(Q1[:, :, :], XQ[:, :, :], ROUND, ROUND, ALU.add, ALU.subtract)\
                    .then_inc(s_q1, 1)

            def gated(b, j):
                t, i = j // 2, j % 2
                n = 4 * b + j
                dve.wait_ge(s_tg, n + 1)
                dve.scalar_tensor_tensor(out=SG[:, j % 2, :], in0=TG[:, j % 2, :], scalar=1.0,
                                         in1=R[0][:, :], op0=ALU.add, op1=ALU.mult)\
                    .then_inc(s_sg, 1)
                dve.wait_ge(s_sg, n + 1)
                if b > 0:
                    dve.wait_ge(s_q2, 2 * b)
                dve.tensor_tensor(XM[:, t, 4 * i:4 * i + 4, :], SG[:, j % 2, :].rearrange("p (c l) -> p c l", c=4),
                                  R[1][:, :].rearrange("p (c l) -> p c l", c=4), ALU.mult)\
                    .then_inc(s_xm, 1)

            def stage_b(b, t):
                dve.wait_ge(s_hA, 4 * b + 2 * t + 2)
                if b > 0:
                    dve.wait_ge(s_XT, 4 * b)
                a = HA[:, t, :, :].rearrange("p (a b e) l -> p a b (e l)", a=2, b=2)
                o = HB[:, t, :, :].rearrange("p (a b e) l -> p a b (e l)", a=2, b=2)
                dve.tensor_tensor(o[:, :, 0, :], a[:, :, 0, :], a[:, :, 1, :], ALU.add).then_inc(s_hB, 1)
                dve.tensor_tensor(o[:, :, 1, :], a[:, :, 0, :], a[:, :, 1, :], ALU.subtract).then_inc(s_hB, 1)

            def scales2(b, t):
                n = 10 * b + 5 * t
                for i in range(2):
                    j = 2 * t + i
                    dve.wait_ge(s_Y, 4 * b + j + 1)
                    dve.tensor_reduce(AM2[:, t, i:i + 1], R[i][:, :], AX.X, ALU.max,
                                      apply_absolute_value=True).then_inc(s_am2, 1)
                dve.wait_ge(s_am2, 4 * b + 2 * t + 2)
                if b > 0:
                    dve.wait_ge(s_x2, 2 * b)
                dve.tensor_tensor(AMX[:, t:t + 1], AM2[:, t, 0:1], AM2[:, t, 1:2], ALU.max).then_inc(s_qs2, 1)
                dve.wait_ge(s_qs2, n + 1)
                dve.tensor_scalar(AMT[:, t:t + 1], AMX[:, t:t + 1], KK[:, t:t + 1], EPS0, ALU.mult, ALU.max)\
                    .then_inc(s_qs2, 1)
                dve.wait_ge(s_qs2, n + 2)
                dve.reciprocal(RC2[:, t:t + 1], AMT[:, t:t + 1]).then_inc(s_qs2, 1)
                dve.tensor_scalar(DSC[:, t:t + 1], AMT[:, t:t + 1], WSC[:, 2:3], None, ALU.mult)\
                    .then_inc(s_qs2, 1)
                dve.wait_ge(s_qs2, n + 4)
                dve.tensor_scalar(QS2[:, t:t + 1], RC2[:, t:t + 1], KK[:, t:t + 1], QB, ALU.mult, ALU.mult)\
                    .then_inc(s_qs2, 1)

            def quant2(b, t):
                dve.wait_ge(s_yq, 4 * b + 2 * t + 2)
                if b > 0:
                    dve.wait_ge(s_q2T, 2 * b)
                dve.tensor_scalar(Q2[:, t, :], YQ[:, t, :], ROUND, QB - 1, ALU.subtract, ALU.min)\
                    .then_inc(s_q2, 1)

            def rows_x2(b):
                if b > 0:
                    dve.wait_ge(s_o, 2 * b)
                for t in range(T):
                    dve.wait_ge(s_dn, 2 * b + t + 1)
                    dve.scalar_tensor_tensor(out=X2[:, t, :], in0=R[t][:, 0:D],
                                             scalar=DSC[:, t:t + 1], in1=X1[:, t, :], op0=ALU.mult,
                                             op1=ALU.add).then_inc(s_x2, 1)
                dve.wait_ge(s_x2, 2 * (b + 1))
                norm_stats(2, b, X2, 1.0, EPS0)

            def x2_rows(b):
                if b > 0:
                    dve.wait_ge(s_x3T, b)
                norm_rows(2, b, X2, XN2, s_xn2)

            def rows_x3(b):
                dve.wait_ge(s_pxm, b + 1)
                dve.tensor_tensor(X3[:, :, :], R[2][:, :].rearrange("p (t d) -> p t d", t=T), X2[:, :, :],
                                  ALU.add).then_inc(s_x3, 1)
                dve.wait_ge(s_x3, b + 1)
                norm_stats(3, b, X3, 1.0 + EPS1, EPS0 * EPS1)

            def scales3(b):
                dve.wait_ge(s_x2T, b + 1)
                norm_rows(3, b, X3, D3, s_d3)
                a = 5 * b
                dve.wait_ge(s_d3, 2 * (b + 1))
                if b > 0:
                    dve.wait_ge(s_h, 4 * b)
                dve.tensor_reduce(GM[:, :], D3[:, :, :], AX.X, ALU.max, apply_absolute_value=True)\
                    .then_inc(s_gm, 1)
                dve.wait_ge(s_gm, a + 1)
                dve.reciprocal(GI[:, :], GM[:, :]).then_inc(s_gm, 1)
                dve.tensor_scalar(NG[:, :], GM[:, :], -1.0, None, ALU.mult).then_inc(s_gm, 1)
                dve.wait_ge(s_gm, a + 3)
                dve.tensor_tensor(GN[:, :], GM[:, :], GI[:, :], ALU.mult).then_inc(s_gm, 1)
                dve.wait_ge(s_gm, a + 4)
                dve.tensor_scalar(S1[:, :], GN[:, :], WMEAN[:, 3:4], None, ALU.mult).then_inc(s_gm, 1)
                for t in range(T):
                    i = dve.tensor_scalar(C3[:, t, :], D3[:, t, :], GM[:, t:t + 1], NG[:, t:t + 1],
                                          ALU.min, ALU.max)
                i.then_inc(s_c3, 1)

            def hidden_stats(b, j):
                t, i = j // 2, j % 2
                dve.wait_ge(s_h, 4 * b + j + 1)
                dve.bn_stats(ST3[:, t, i, :], HG[:, t, i * 512:(i + 1) * 512]).then_inc(s_st3, 1)

            def hidden_norm(b, t):
                dve.wait_ge(s_st3, 4 * b + 2 * t + 2)
                dve.bn_aggr(MV3[:, t, :], ST3[:, t, :, :].rearrange("p a b -> p (a b)")).then_inc(s_mv3, 1)
                dve.wait_ge(s_mv3, 6 * b + 3 * t + 1)
                dve.tensor_scalar(NM3[:, t:t + 1], MV3[:, t, 0:1], -1.0, None, ALU.mult).then_inc(s_mv3, 1)
                dve.tensor_scalar(VE3[:, t:t + 1], MV3[:, t, 1:2], EPS1, None, ALU.add).then_inc(s_mv3, 1)

            def hidden_range(b, t):
                n = 10 * b + 5 * t
                dve.wait_ge(s_hd, 2 * b + t + 1)
                dve.tensor_reduce(GM2[:, t:t + 1], HD[:, t, :], AX.X, ALU.max, apply_absolute_value=True)\
                    .then_inc(s_gm2, 1)
                dve.wait_ge(s_gm2, n + 1)
                dve.tensor_scalar(NG2[:, t:t + 1], GM2[:, t:t + 1], -1.0, None, ALU.mult).then_inc(s_gm2, 1)
                dve.reciprocal(GI2[:, t:t + 1], GM2[:, t:t + 1]).then_inc(s_gm2, 1)
                dve.wait_ge(s_gm2, n + 3)
                dve.tensor_tensor(GN2[:, t:t + 1], GM2[:, t:t + 1], GI2[:, t:t + 1], ALU.mult).then_inc(s_gm2, 1)
                dve.wait_ge(s_gm2, n + 4)
                dve.tensor_scalar(S2[:, t:t + 1], GN2[:, t:t + 1], WMEAN[:, 4:5], None, ALU.mult)\
                    .then_inc(s_gm2, 1)

            def hidden_clip(b, t):
                dve.wait_ge(s_gm2, 10 * b + 5 * t + 2)
                dve.tensor_scalar(HC[:, t, :], HD[:, t, :], GM2[:, t:t + 1], NG2[:, t:t + 1],
                                  ALU.min, ALU.max).then_inc(s_hc, 1)

            def rows_out(b, t):
                dve.wait_ge(s_pj, 2 * b + t + 1)
                dve.wait_ge(s_gm2, 10 * b + 5 * t + 5)
                if b > 0:
                    dve.wait_ge(d_out[b - 1], 16 * T)
                dve.scalar_tensor_tensor(out=XO[:, t, :], in0=R[2][:, 0:D],
                                         scalar=S2[:, t:t + 1], in1=X3[:, t, :], op0=ALU.mult,
                                         op1=ALU.add).then_inc(s_o, 1)

            dve.memset(CT[:, :, 0:TAPS - 1], 0.0).then_inc(s_const, 1)
            dve.memset(ONES[:, :], 1.0).then_inc(s_const, 1)
            dve.memset(ROUNDC[:, :], ROUND).then_inc(s_const, 1)
            dve.memset(DA[:, :, :, 0], 0.0).then_inc(s_const, 1)
            dve.wait_ge(d_in, 16)
            dve.wait_ge(d_cw, 16)
            dve.tensor_tensor(WCONV[:, :, :], CW, INW[:, :].unsqueeze(1).to_broadcast([P, TAPS, D]),
                              ALU.mult).then_inc(s_wconv, 1)
            dve.wait_ge(d_vec, 48)
            dve.tensor_scalar(HALF[:, 0, :], VEC[:, 0, :], 0.5, None, ALU.mult).then_inc(s_wconv, 1)
            dve.tensor_scalar(HALF[:, 1, :], VEC[:, 2, :], 0.5, None, ALU.mult).then_inc(s_wconv, 1)

            def z_stats(b):
                dve.wait_ge(d_x[b], 16)
                norm_stats(0, b, X[:, b, :, :], 1.0, EPS0)

            def z_rows(b):
                norm_rows(0, b, X[:, b, :, :], ZN, s_zn)

            plan = []
            for n in range(STEPS):
                plan += [(drive, SP["drive"][n], n), (scan, SP["scan"][n], n), (read_out, SP["read"][n], n)]
            plan += [(prep_u, SP["u"]), (prep_split, SP["split"]), (prep_softplus1, SP["sp1"]),
                     (prep_softplus2, SP["sp2"]), (z_stats, SP["zs"]), (z_rows, SP["zr"]), (prep_sz, SP["sz"]),
                     (attn_max, SP["amax"]), (attn_norm, SP["anorm"])]
            plan += [(rows_out, SP["out"][t], t) for t in range(T)]
            plan += [(gate_y, SP["gate_y"]), (rows_x1, SP["x1"]), (quant1, SP["quant1"])]
            plan += [(gated, SP["gated"][j], j) for j in range(4)]
            plan += [(stage_b, SP["stage_b"][t], t) for t in range(T)]
            plan += [(scales2, SP["scales2"][t], t) for t in range(T)]
            plan += [(quant2, SP["quant2"][t], t) for t in range(T)]
            plan += [(rows_x2, SP["x2"]), (x2_rows, SP["x2r"]), (rows_x3, SP["x3"]), (scales3, SP["scales3"])]
            plan += [(hidden_stats, SP["hstats"][j], j) for j in range(4)]
            for t in range(T):
                plan += [(hidden_norm, SP["hnorm"][t], t), (hidden_range, SP["hrange"][t], t),
                         (hidden_clip, SP["hclip"][t], t)]
            for u in range(-SPOTS, SPOTS * (B + 4)):
                if u == SP["sel"]:
                    dve.wait_ge(d_sel, 16)
                    dve.tensor_copy(SEL[:, :, :], SELC[:, :].unsqueeze(2).to_broadcast([96, 32, P]))\
                        .then_inc(s_sel, 1)
                if u == SP["eyeb"]:
                    dve.wait_ge(d_eye, 16)
                    dve.tensor_copy(EYEB[:, :], EYE[:, :]).then_inc(s_eyeb, 1)
                if u == SP["aneg"]:
                    dve.wait_ge(s_aexp, 1)
                    dve.tensor_scalar(ANEG[:, :, :], AEXP[:, :, :], -1.0, None, ALU.mult).then_inc(s_aneg, 1)
                if u == SP["wscale"][0]:
                    weight_scales(0, 3)
                if u == SP["wscale"][1]:
                    weight_scales(3, 2)
                for i in range(5):
                    if u == SP["wter"][i]:
                        weight_ternary(i)
                for fn, spot, *args in plan:
                    b, r = divmod(u - spot, SPOTS)
                    if r == 0 and 0 <= b < B:
                        fn(b, *args)

        @block.gpsimd
        def _(pool):
            def root(b, i):
                pool.wait_ge(s_lnst[i], 5 * (b + 1))
                pool.tensor_tensor(RS[:, i, :], VE[:, i, :], MHALF[:, 0:T], ALU.pow).then_inc(s_rstd[i], 1)

            def sum_pair(b, s):
                g, q, c = STEPS * b + s, s // T, s % T
                pool.wait_ge(s_z, g + 1)
                if q == 0 and b > 0:
                    pool.wait_ge(s_fold, 2 * (b - 1) + c + 1)
                if q > 1:
                    pool.wait_ge(s_acc, 6 * b + s - 3)
                dst = ACC if q == 0 else PAIR
                pool.tensor_tensor(dst[:, c, :, :], Z[:, g % NZ, 0:2, :], Z[:, g % NZ, 2:4, :],
                                   ALU.add).then_inc(s_pair, 1)
                if q > 0:
                    pool.wait_ge(s_pair, g + 1)
                    pool.tensor_tensor(ACC[:, c, :, :], ACC[:, c, :, :], PAIR[:, c, :, :],
                                       ALU.add).then_inc(s_acc, 1)

            def fold(b, c):
                pool.wait_ge(s_acc, 6 * b + 5 + c)
                if b > 0:
                    pool.wait_ge(s_v, 3 * b)
                pool.tensor_tensor(YS[:, c, :], ACC[:, c, 0, :], ACC[:, c, 1, :], ALU.add).then_inc(s_fold, 1)

            def stage_a(b, t):
                pool.wait_ge(s_xm, 4 * b + 2 * t + 2)
                if b > 0:
                    pool.wait_ge(s_dn, 2 * b)
                for i, op in enumerate((ALU.add, ALU.subtract)):
                    pool.tensor_tensor(HA[:, t, 4 * i:4 * i + 4, :], XM[:, t, 0:4, :], XM[:, t, 4:8, :], op)\
                        .then_inc(s_hA, 1)

            def hidden_rows(b, t):
                pool.wait_ge(s_mv3, 6 * b + 3 * t + 3)
                pool.tensor_tensor(RS3[:, t:t + 1], VE3[:, t:t + 1], MHALF[:, 0:1], ALU.pow).then_inc(s_rs3, 1)
                pool.wait_ge(s_rs3, 2 * b + t + 1)
                pool.tensor_tensor(MR3[:, t:t + 1], NM3[:, t:t + 1], RS3[:, t:t + 1], ALU.mult).then_inc(s_mr3, 1)
                pool.wait_ge(s_mr3, 2 * b + t + 1)
                pool.tensor_scalar(HD[:, t, :], HG[:, t, :], RS3[:, t:t + 1], MR3[:, t:t + 1],
                                   ALU.mult, ALU.add).then_inc(s_hd, 1)

            pool.memset(MHALF[:, :], -0.5).then_inc(s_mhalf, 1)
            pool.wait_ge(s_mhalf, 1)
            plan = [(sum_pair, SP["sum"][n], n) for n in range(STEPS)]
            plan += [(fold, SP["fold"][c], c) for c in range(T)]
            plan += [(root, SP["root"][i], i) for i in range(4)]
            plan += [(stage_a, SP["stage_a"][t], t) for t in range(T)]
            plan += [(hidden_rows, SP["hrows"][t], t) for t in range(T)]
            for u in range(-SPOTS, SPOTS * (B + 4)):
                for fn, spot, *args in plan:
                    b, r = divmod(u - spot, SPOTS)
                    if r == 0 and 0 <= b < B:
                        fn(b, *args)


_NAMES = ["x", "ctxT", "inproj", "convw", "convb", "xprojT", "dtprojT", "dtb", "alog", "dskip", "wgate", "wup",
          "wdown", "wq", "wk", "bq", "bk", "wfc", "wproj", "eye", "had", "sel"]


def kernel(**inputs):
    import concourse.bacc as bacc
    from concourse.bass_utils import run_bass_kernel_spmd

    a = {k: np.asarray(v) for k, v in inputs.items()}

    def rows(v):
        return v.reshape(B, T, P, -1).transpose(2, 0, 1, 3)

    def halves(v):
        return np.moveaxis(v.reshape((-1, P) + v.shape[1:]), 1, 0)

    def weight(w):
        return halves(w.T).reshape(P, -1)

    xp = a["L0_xattn_x_proj_w"]
    xp = np.concatenate([xp[RANK:], xp[RANK:], xp[RANK:], xp[:RANK]], axis=0)
    h = np.ones((1, 1), np.float32)
    while h.shape[0] < P:
        h = np.block([[h, h], [h, -h]])
    eye = np.eye(P, dtype=np.float32)
    import ml_dtypes
    arrays = {
        "x": rows(a["x"]),
        "ctxT": a["ctx_1024"].transpose(2, 0, 1),
        "inproj": a["L0_xattn_in_proj_w"].T,
        "convw": a["L0_xattn_conv_w"][:, 0, :].T.reshape(1, TAPS, D)[0],
        "convb": halves(a["L0_xattn_conv_b"]),
        "xprojT": halves(xp.T),
        "dtprojT": a["L0_xattn_dt_proj_w"].T,
        "dtb": halves(a["L0_xattn_dt_proj_b"]),
        "alog": halves(a["L0_xattn_A_log"]),
        "dskip": halves(a["L0_xattn_D"]),
        "wgate": weight(a["L0_ffn_w_gate"]),
        "wup": weight(a["L0_ffn_w_up"]),
        "wdown": weight(a["L0_ffn_w_down"]),
        "wq": a["L1_xattn_Wq"].T,
        "wk": a["L1_xattn_Wk"].T,
        "bq": a["L1_xattn_bq"].reshape(P, 1),
        "bk": a["L1_xattn_bk"].reshape(P, 1),
        "wfc": weight(a["L1_ffn_w_fc"]).reshape(P, 2, FF),
        "wproj": weight(a["L1_ffn_w_proj"]).reshape(P, G8, D),
        "eye": eye,
        "had": np.stack([np.concatenate([h, h], 1), np.concatenate([h, -h], 1)], axis=1),
        "sel": np.tile(np.eye(32, dtype=np.float32), (3, 1)).astype(ml_dtypes.bfloat16),
    }
    nc = bacc.Bacc("TRN2", target_bir_lowering=False, num_devices=1)
    feed, args = {}, []
    for name in _NAMES:
        v = np.ascontiguousarray(arrays[name])
        feed[f"in_{name}"] = v
        args.append(nc.dram_tensor(f"in_{name}", v.shape, mybir.dt.from_np(v.dtype), kind="ExternalInput").ap())
    args.append(nc.dram_tensor("out_0", (P, B, T, D), F32, kind="ExternalOutput").ap())
    build(nc, *args)
    r = run_bass_kernel_spmd(nc, [feed], core_ids=[0])
    y = r.results[0]["out_0"]
    return np.ascontiguousarray(y.transpose(1, 2, 0, 3).reshape(B, L, D))
```
